# Optimizing a Trainium2 kernel written in Bass

```python
import numpy as np
import jax
import jax.numpy as jnp

def _softmax(x, axis=-1):
    return jax.nn.softmax(x, axis=axis)

def _gelu(x):
    return jax.nn.gelu(x, approximate=True)

def _silu(x):
    return jax.nn.silu(x)

def _sigmoid(x):
    return jax.nn.sigmoid(x)

def _layernorm(x, axis=-1, eps=1e-05):
    m = jnp.mean(x, axis=axis, keepdims=True)
    v = jnp.var(x, axis=axis, keepdims=True)
    return (x - m) / jnp.sqrt(v + eps)

def _scatter_add(tgt, idx, src, axis=0):
    return tgt.at[idx].add(src)

def _segment_sum(src, seg, n):
    return jax.ops.segment_sum(src, seg, n)
kernel_name = 'mk_early_fusion_d1_tok_img1024_r4_bf4429'

def setup_inputs(seed: int=0):
    np.random.seed(seed)
    _w = jnp.asarray

    def _rec_inputs():
        import jax
        import jax.numpy as jnp
        _rk = jax.random.key(seed)
        x = -0.00016672 + 0.999947 * jax.random.normal(jax.random.fold_in(_rk, 1), (64, 3, 96, 96), jnp.float32)
        txt = 0.0018035 + 1.41312 * jax.random.normal(jax.random.fold_in(_rk, 2), (64, 32, 256), jnp.float32)
        return (x, txt)
    x, txt = _rec_inputs()

    def _L0_tok_setup():
        import jax, jax.numpy as jnp
        import numpy as np
        IMG = 96
        PATCH = 16
        CIN = 3
        EMBED = 256
        NP_ = (IMG // PATCH) ** 2
        key = jax.random.key(seed)
        k1, k2, k3, k4, k5 = jax.random.split(key, 5)
        x = jax.random.normal(k1, (64, CIN, IMG, IMG), dtype=jnp.float32)
        d_in = PATCH * PATCH * CIN
        W = jax.random.normal(k2, (d_in, EMBED), dtype=jnp.float32) / np.sqrt(d_in)
        b = jax.random.normal(k3, (EMBED,), dtype=jnp.float32) * 0.01
        class_token = jax.random.normal(k4, (1, 1, EMBED), dtype=jnp.float32)
        pos_emb = jax.random.normal(k5, (1, NP_ + 1, EMBED), dtype=jnp.float32)
        return {'x': x, 'W': W, 'b': b, 'class_token': class_token, 'pos_emb': pos_emb}
    _L0_tok_all = _L0_tok_setup()
    _L0_tok_in = {k: v for k, v in _L0_tok_all.items() if k in ('W', 'b', 'class_token', 'pos_emb')}
    del _L0_tok_all

    def _L0_attn_setup():
        import jax, jax.numpy as jnp
        import numpy as np
        B, S, D, H = (2, 512, 256, 16)
        HD = D // H
        key = jax.random.key(seed)
        ks = jax.random.split(key, 5)
        scale = 1.0 / np.sqrt(D)
        x = jax.random.normal(ks[0], (B, S, D), dtype=jnp.float32)
        W_Q = jax.random.uniform(ks[1], (D, D), jnp.float32, -scale, scale)
        W_K = jax.random.uniform(ks[2], (D, D), jnp.float32, -scale, scale)
        W_V = jax.random.uniform(ks[3], (D, D), jnp.float32, -scale, scale)
        W_O = jax.random.uniform(ks[4], (D, D), jnp.float32, -scale, scale)
        return {'x': x, 'W_Q': W_Q, 'W_K': W_K, 'W_V': W_V, 'W_O': W_O}
    _L0_attn_all = _L0_attn_setup()
    _L0_attn_in = {k: v for k, v in _L0_attn_all.items() if k in ('W_Q', 'W_K', 'W_V', 'W_O')}
    del _L0_attn_all

    def _L0_ffn_setup():
        import jax, jax.numpy as jnp
        import numpy as np
        D_MODEL = 256
        HIDDEN = 1024
        NUM_EXPERTS = 8
        TOP_K = 2
        key = jax.random.key(seed)
        k_x, k_g, k_in, k_out = jax.random.split(key, 4)
        bound_in = 1.0 / HIDDEN
        bound_out = 1.0 / D_MODEL
        x = jax.random.normal(k_x, (2, 512, D_MODEL), dtype=jnp.float32)
        w_gate = jax.random.uniform(k_g, (NUM_EXPERTS, D_MODEL), dtype=jnp.float32, minval=-D_MODEL ** (-0.5), maxval=D_MODEL ** (-0.5))
        w_in = jax.random.uniform(k_in, (NUM_EXPERTS, HIDDEN, D_MODEL), dtype=jnp.float32, minval=-bound_in, maxval=bound_in)
        w_out = jax.random.uniform(k_out, (NUM_EXPERTS, D_MODEL, HIDDEN), dtype=jnp.float32, minval=-bound_out, maxval=bound_out)
        return {'x': x, 'w_gate': w_gate, 'w_in': w_in, 'w_out': w_out}
    _L0_ffn_all = _L0_ffn_setup()
    _L0_ffn_in = {k: v for k, v in _L0_ffn_all.items() if k in ('w_gate', 'w_in', 'w_out')}
    del _L0_ffn_all
    return {'x': x, 'txt': txt, 'L0_tok_W': _L0_tok_in['W'], 'L0_tok_b': _L0_tok_in['b'], 'L0_tok_class_token': _L0_tok_in['class_token'], 'L0_tok_pos_emb': _L0_tok_in['pos_emb'], 'L0_attn_W_Q': _L0_attn_in['W_Q'], 'L0_attn_W_K': _L0_attn_in['W_K'], 'L0_attn_W_V': _L0_attn_in['W_V'], 'L0_attn_W_O': _L0_attn_in['W_O'], 'L0_ffn_w_gate': _L0_ffn_in['w_gate'], 'L0_ffn_w_in': _L0_ffn_in['w_in'], 'L0_ffn_w_out': _L0_ffn_in['w_out']}

def reference(x, txt, L0_tok_W, L0_tok_b, L0_tok_class_token, L0_tok_pos_emb, L0_attn_W_Q, L0_attn_W_K, L0_attn_W_V, L0_attn_W_O, L0_ffn_w_gate, L0_ffn_w_in, L0_ffn_w_out):
    import jax
    import jax.numpy as jnp

    def _L0_tok_ref(x, W, b, class_token, pos_emb):
        import jax, jax.numpy as jnp
        import numpy as np
        IMG = 96
        PATCH = 16
        CIN = 3
        EMBED = 256
        NP_ = (IMG // PATCH) ** 2
        B = x.shape[0]
        Hp = IMG // PATCH
        patches = x.reshape(B, CIN, Hp, PATCH, Hp, PATCH)
        patches = patches.transpose(0, 2, 4, 1, 3, 5).reshape(B, Hp * Hp, CIN * PATCH * PATCH)
        patch_emb = jnp.einsum('bnd,de->bne', patches, W) + b
        cls = jnp.broadcast_to(class_token, (B, 1, EMBED))
        emb = jnp.concatenate([cls, patch_emb], axis=1) + pos_emb
        return emb

    def _L0_attn_ref(x, W_Q, W_K, W_V, W_O):
        import jax, jax.numpy as jnp
        import numpy as np
        B, S, D, H = (2, 512, 256, 16)
        HD = D // H
        b, s, d = x.shape
        Q = (x @ W_Q.T).reshape(b, s, H, HD).transpose(0, 2, 1, 3)
        K = (x @ W_K.T).reshape(b, s, H, HD).transpose(0, 2, 1, 3)
        V = (x @ W_V.T).reshape(b, s, H, HD).transpose(0, 2, 1, 3)
        attn = jnp.einsum('bhqd,bhkd->bhqk', Q, K) / jnp.sqrt(jnp.float32(HD))
        slopes = 1.0 / (2.0 ** 8) ** ((jnp.arange(H, dtype=jnp.float32) + 1) / H)
        pos = jnp.arange(s)
        rel = jnp.minimum(pos[None, :] - pos[:, None], 0).astype(jnp.float32)
        bias = slopes[:, None, None] * rel[None, :, :]
        causal = pos[None, :] <= pos[:, None]
        attn = jnp.where(causal[None, None], attn + bias[None], -jnp.inf)
        attn = jax.nn.softmax(attn, axis=-1)
        out = jnp.einsum('bhqk,bhkd->bhqd', attn, V)
        out = out.transpose(0, 2, 1, 3).reshape(b, s, d)
        return out @ W_O.T

    def _L0_ffn_ref(x, w_gate, w_in, w_out):
        import jax, jax.numpy as jnp
        import numpy as np
        D_MODEL = 256
        HIDDEN = 1024
        NUM_EXPERTS = 8
        TOP_K = 2
        B, S, D = x.shape
        E = w_in.shape[0]
        xt = x.reshape(-1, D)
        logits = (xt @ w_gate.T).astype(jnp.float32)
        top_logits, top_idx = jax.lax.top_k(logits, TOP_K)
        top_gates = jax.nn.softmax(top_logits, axis=-1).astype(x.dtype)
        gates = (jax.nn.one_hot(top_idx, E, dtype=x.dtype) * top_gates[..., None]).sum(axis=1)
        y = jnp.zeros_like(xt)
        for e in range(E):
            h = xt @ w_in[e].T
            y = y + gates[:, e:e + 1] * (h @ w_out[e].T)
        return y.reshape(B, S, D)
    h = _L0_tok_ref(x, L0_tok_W, L0_tok_b, L0_tok_class_token, L0_tok_pos_emb)
    h = jnp.concatenate([h, txt], axis=1)
    h = h + _L0_attn_ref(_layernorm(h, axis=-1), L0_attn_W_Q, L0_attn_W_K, L0_attn_W_V, L0_attn_W_O)
    h = h + _L0_ffn_ref(_layernorm(h, axis=-1), L0_ffn_w_gate, L0_ffn_w_in, L0_ffn_w_out)
    return h

_drawn_inputs = setup_inputs


def setup_inputs(seed=0):
    import zlib

    import numpy as np

    out = dict(_drawn_inputs(seed))
    spreads = {}
    factors = {'L0_tok_b': 8.0, 'L0_ffn_w_gate': 8.0, 'L0_ffn_w_in': 8.0, 'L0_ffn_w_out': 8.0}
    for name, (base, spread) in spreads.items():
        noise = np.random.default_rng([zlib.crc32(name.encode()), seed]).standard_normal(out[name].shape)
        drawn = base * np.exp(spread * noise) if base else spread * noise
        out[name] = jnp.asarray(drawn.astype(out[name].dtype))
    for name, factor in factors.items():
        out[name] = (out[name] * factor).astype(out[name].dtype)
    return out
```

```python
from contextlib import ExitStack

import concourse.bass as bass
from concourse import mybir

ALU = mybir.AluOpType
ACT = mybir.ActivationFunctionType
AX_X = mybir.AxisListType.X
F32 = mybir.dt.float32
F32R = mybir.dt.float32r
BF16 = mybir.dt.bfloat16
U32 = mybir.dt.uint32

P = 128
B, CIN, IMG, PATCH = 64, 3, 96, 16
NPATCH = (IMG // PATCH) ** 2
TXT = 32
S = 1 + NPATCH + TXT
D, H, E, HID = 256, 16, 8, 1024
HD = D // H
DC = D // P
KP = CIN * PATCH * PATCH // P
JC = HID // P
EPS = 1e-5

TILES = (S + 1) // 2
PATCH_TILES = NPATCH // 2
XSLOT = 6
SP1 = S + 1

HC = H // DC
QUAD = 4
GS = 4
GT = GS * S
GROUPS = B // GS
STEPS = GS * DC
VW = 2 * HD + 2
NBIAS = S + 6
DVE_E = 4


def after(engine, semaphore, value):
    if isinstance(value, int) and value <= 0:
        return
    engine.wait_ge(semaphore, value)


def fusion_block(nc, x_t, base, posb, sel, w_patch, w_qkv, w_o, w_g, w_in, w_out, ident_d, bias_l_d, bias_r_d,
                 head_mask_d, iota_d, out):
    ctx = ExitStack()
    with ctx:
        def sb(name, shape, dt=F32):
            return ctx.enter_context(nc.sbuf_tensor(name, shape, dt))

        def sem(name):
            return ctx.enter_context(nc.semaphore(name))

        hid = sb("hid", [P, TILES, D])
        feat = sb("feat", [P, DC, B, S])
        feat_flat = feat[:].rearrange("p c b t -> p c (b t)")
        feat_tb = feat[:].rearrange("p c b t -> p c t b")
        ident = sb("ident", [P, P])
        wqkv_hi, wqkv_lo = sb("wqkv_hi", [P, DC, 3 * D], F32R), sb("wqkv_lo", [P, DC, 3 * D], F32R)
        wo_hi, wo_lo = sb("wo_hi", [P, DC, D], F32R), sb("wo_lo", [P, DC, D], F32R)
        wg_hi, wg_lo = sb("wg_hi", [P, DC, E], F32R), sb("wg_lo", [P, DC, E], F32R)
        me_hi, me_lo = sb("me_hi", [P, DC, E, D], F32R), sb("me_lo", [P, DC, E, D], F32R)
        head_mask = sb("head_mask", [P, HC])
        iota = sb("iota", [P, E])
        bias_l = sb("bias_l", [NBIAS, S], BF16)
        bias_r = sb("bias_r", [NBIAS, H * SP1], BF16)
        win_s = sb("win_s", [P, JC, D])
        wout_s = sb("wout_s", [P, JC, D])
        stats = sb("stats", [P, 2, 6])
        mv = sb("mv", [P, 2, 2])
        rstd = sb("rstd", [P, 2])
        root = sb("root", [P, 3, 2])
        normed = sb("normed", [P, 2, D])
        gtmp = sb("gtmp", [P, 8, E])
        gidx = sb("gidx", [P, E], U32)
        psum = ctx.enter_context(nc.psum_tensor("psum", [P, 8, 512], F32))

        w_in_sem = sem("patch_weights_in")
        c_in = sem("constants_in")
        wq_in = sem("attention_weights_in")
        base_in = sem("base_in")
        x_in = [sem(f"x_in{n}") for n in range(XSLOT // 2)]
        emb_ready, emb_read = sem("emb_ready"), sem("emb_read")
        hid_ready = sem("hid_ready")
        dve_chain = sem("dve_chain")
        stats1, stats3, aggr_ready = sem("stats1_ready"), sem("stats3_ready"), sem("aggr_ready")
        var_ready, log_ready, guess_ready = sem("var_ready"), sem("log_ready"), sem("guess_ready")
        normed_ready, normed_used = sem("normed_ready"), sem("normed_used")
        feat_ready = sem("feat_ready")
        w_hi_ready, w_lo_ready = sem("w_hi_ready"), sem("w_lo_ready")
        pads_ready = sem("pads_ready")

        exp_in = sem("expert_in")
        xs_hi, xs_lo = sem("xs_hi"), sem("xs_lo")
        proj_ready = sem("proj_ready")
        proj_hi = sem("proj_hi")
        q_ready, k_ready, vt_ready, v_ready = sem("q_ready"), sem("k_ready"), sem("vt_ready"), sem("v_ready")
        ot_ready, me_ready, me_hi_done, me_done = sem("ot_ready"), sem("me_ready"), sem("me_hi_done"), sem("me_done")
        ot_done = sem("ot_done")
        kbd_ready = sem("kbd_ready")
        s_ready, max_done, shifted_ready = sem("s_ready"), sem("max_done"), sem("shifted_ready")
        probs_ready, pt_ready, pt_hi_done, pt_lo_done = (sem("probs_ready"), sem("pt_ready"), sem("pt_hi_done"),
                                                         sem("pt_lo_done"))
        pv_ready, otmp_ready, o_read, on_ready = sem("pv_ready"), sem("otmp_ready"), sem("o_read"), sem("on_ready")

        of_hi, of_lo = sem("of_hi"), sem("of_lo")
        wo_ready, mid_ready = sem("wo_ready"), sem("mid_ready")
        n2_ready, x2t_ready, x2_hi, x2_lo = sem("n2_ready"), sem("x2t_ready"), sem("x2_hi_done"), sem("x2_lo_done")
        g_ready, g_read, gd_ready, ge_ready, gates_ready = (sem("g_ready"), sem("g_read"), sem("gd_ready"),
                                                            sem("ge_ready"), sem("gates_ready"))
        moe_ready, moe_read = sem("moe_ready"), sem("moe_read")
        scaled_ready, part_ready, sum_ready = sem("scaled_ready"), sem("part_ready"), sem("sum_ready")
        out_done = sem("out_done")

        early = ExitStack()
        xs = early.enter_context(nc.sbuf_tensor("xs", [P, XSLOT, KP, P], F32))
        wp = early.enter_context(nc.sbuf_tensor("wp", [P, KP, D], F32))
        posb_s = early.enter_context(nc.sbuf_tensor("posb_s", [3, TILES, D], F32))
        sel_s = early.enter_context(nc.sbuf_tensor("sel_s", [3, 2, P], F32))
        raw_qkv = early.enter_context(nc.sbuf_tensor("raw_qkv", [P, DC, 3 * D], F32))
        raw_o = early.enter_context(nc.sbuf_tensor("raw_o", [P, DC, D], F32))
        raw_g = early.enter_context(nc.sbuf_tensor("raw_g", [P, DC, E], F32))
        early.close()
        late = ExitStack()

        def lsb(name, shape, dt=F32):
            return late.enter_context(nc.sbuf_tensor(name, shape, dt))

        of_h, of_l = lsb("of_h", [P, 2, DC, P], F32R), lsb("of_l", [P, 2, DC, P], F32R)
        x2_h, x2_l = lsb("x2_h", [P, 2, DC, P], F32R), lsb("x2_l", [P, 2, DC, P], F32R)
        scaled = lsb("scaled", [P, E - DVE_E, D])
        part = lsb("part", [P, 2, D])
        late.close()
        mid = ExitStack()

        def msb(name, shape, dt=F32):
            return mid.enter_context(nc.sbuf_tensor(name, shape, dt))

        xg_hi, xg_lo = msb("xg_hi", [P, DC, GT], F32R), msb("xg_lo", [P, DC, GT], F32R)
        qt_hi, qt_lo = msb("qt_hi", [P, 2, DC, GT], F32R), msb("qt_lo", [P, 2, DC, GT], F32R)
        kt_hi, kt_lo = msb("kt_hi", [P, 2, DC, GS, SP1], F32R), msb("kt_lo", [P, 2, DC, GS, SP1], F32R)
        vt = msb("vt", [P, DC, GT])
        v2 = msb("v2", [S, 2, GS, H, VW], F32R)
        kbd_hi, kbd_lo = msb("kbd_hi", [P, DC, HC, SP1], F32R), msb("kbd_lo", [P, DC, HC, SP1], F32R)
        rowmax = msb("rowmax", [S, 2, HC])
        probs = msb("probs", [S, 2, HC * SP1])
        pt_hi, pt_lo = msb("pt_hi", [S, 2, HC, SP1], F32R), msb("pt_lo", [S, 2, HC, SP1], F32R)
        otmp = msb("otmp", [S, HC, HD])
        osum = msb("osum", [S, HC, HD])
        rden = msb("rden", [S, 2, HC])
        o_nat = msb("o_nat", [S, D])
        mid.close()

        block = ctx.enter_context(nc.Block())

        PAIRS = TILES // 2
        PATCH_PAIRS = PATCH_TILES // 2
        LAST = TILES - 1

        def token_columns(view, pair, j):
            if isinstance(pair, int):
                tile = 2 * pair + j
                if tile == PATCH_TILES:
                    return view[:, :, 0:NPATCH + 2:NPATCH + 1, :]
                if tile == LAST:
                    return view[:, :, S - 1:S, :]
                first = 2 * tile + (1 if tile < PATCH_TILES else 0)
                return view[:, :, first:first + 2, :]
            raise ValueError(pair)

        def looped_columns(view, pair, j, patch):
            return view[:, :, bass.ds(pair * 4 + 2 * j + (1 if patch else 0), 2), :]

        def pairs(engine, step):
            step(0, lambda v, j: token_columns(v, 1, j))
            with engine.Fori(1, PATCH_PAIRS - 1) as n:
                step(n, lambda v, j: looped_columns(v, n + 1, j, True))
            step(PATCH_PAIRS - 1, lambda v, j: token_columns(v, PATCH_PAIRS, j))
            with engine.Fori(PATCH_PAIRS, PAIRS - 1) as n:
                step(n, lambda v, j: looped_columns(v, n + 1, j, False))
            step(PAIRS - 1, lambda v, j: token_columns(v, PAIRS, j))

        E_BANK, T_BANK = 0, XSLOT // 2
        ROUNDS = PATCH_TILES // XSLOT
        PB = XSLOT // 2

        def embed_bank(slot):
            return psum[:, E_BANK + slot, :].rearrange("p (j d) -> p j d", j=2)

        def turned_bank(slot):
            return psum[:, T_BANK + slot, :].rearrange("p (c j r) -> p c j r", c=DC, j=2)

        PT_BANK, O_BANK, M_BANK = 4, 6, 7
        M = psum[:, M_BANK, :]

        def last_bank_free(pe, g, kind, step, last_group=False):
            order = []
            for at in range(STEPS):
                if at % 2 and not (isinstance(g, int) and g == 0 and at == 1):
                    order.append(("out", at))
                if at == 2:
                    order.append(("expert", at))
                if not last_group:
                    order.append(("proj", at))
            at = order.index((kind, step)) if kind else len(order)
            if at:
                kind, step = order[at - 1]
                nxt = g + 1
            else:
                kind, step, nxt = "proj", STEPS - 1, g
            if kind == "out":
                pe.wait_ge(ot_done, g * GS + step // 2)
            elif kind == "expert":
                pe.wait_ge(me_done, g + 1)
            else:
                projected(pe, nxt, step)

        def projected(pe, g, step):
            semaphore = (q_ready, k_ready, vt_ready, v_ready)[step // 2]
            pe.wait_ge(semaphore, g * 2 + (step % 2 + 1))

        def group_pairs(engine, group):
            with engine.Fori(0, (GROUPS - 2) // 2) as r:
                group(r * 2 + 1, 1, r)
                group(r * 2 + 2, 0, r + 1)

        def group_columns(g):
            if isinstance(g, int):
                return feat_flat[:, :, g * GT:(g + 1) * GT]
            return feat_flat[:, :, bass.ds(g * GT, GT)]

        def sample_columns(sample):
            if isinstance(sample, int):
                return feat_flat[:, :, sample * S:(sample + 1) * S]
            return feat_flat[:, :, bass.ds(sample * S, S)]

        def me_slice(t, e, half):
            if isinstance(e, int):
                return t[:, half, e, :]
            return t[:, half, bass.ds(e, 1), :].rearrange("p o d -> p (o d)")

        def pt_banks():
            return psum[0:S, PT_BANK:PT_BANK + 2, 0:QUAD * SP1].rearrange("p b (h q) -> p b h q", q=SP1)[:, :, :, 0:S]

        def o_bank():
            return psum[0:S, O_BANK, 0:HC * VW].rearrange("p (h v) -> p h v", v=VW)

        def hid_tile(n, j, rows=P):
            if isinstance(n, int):
                return hid[0:rows, 2 * n + j, :]
            return hid[0:rows, bass.ds(n * 2 + j, 1), :].rearrange("p o d -> p (o d)")

        @block.sync
        def _(sp):
            sp.dma_start(wp[:], w_patch).then_inc(w_in_sem, 16)
            sp.dma_start(posb_s[:], posb).then_inc(w_in_sem, 16)
            sp.dma_start(sel_s[:], sel).then_inc(w_in_sem, 16)
            for n in range(XSLOT // 2):
                sp.dma_start(xs[:, 2 * n:2 * n + 2], x_t[2 * n:2 * n + 2].rearrange("i p c t -> p i c t")
                             ).then_inc(x_in[n], 16)
            sp.dma_start(ident[:], ident_d).then_inc(c_in, 16)
            sp.dma_start(head_mask[:], head_mask_d).then_inc(c_in, 16)
            sp.dma_start(iota[:], iota_d).then_inc(c_in, 16)
            sp.dma_start(bias_l[:], bias_l_d).then_inc(c_in, 16)
            sp.dma_start(bias_r[:], bias_r_d).then_inc(c_in, 16)
            with sp.Fori(1, PATCH_TILES // XSLOT) as r:
                for n in range(XSLOT // 2):
                    sp.wait_ge(emb_ready, r * PB + (n + 1 - PB))
                    sp.dma_start(xs[:, 2 * n:2 * n + 2],
                                 x_t[bass.ds(r * XSLOT + 2 * n, 2)].rearrange("i p c t -> p i c t")
                                 ).then_inc(x_in[n], 16)
            sp.dma_start(hid[:, PATCH_TILES:LAST, :], base[0:(LAST - PATCH_TILES) * P].rearrange(
                "(i p) d -> p i d", p=P)).then_inc(base_in, 16)
            sp.dma_start(hid[0:B, LAST, :], base[(LAST - PATCH_TILES) * P:]).then_inc(base_in, 16)
            sp.dma_start(raw_qkv[:], w_qkv).then_inc(wq_in, 16)
            sp.dma_start(raw_o[:], w_o).then_inc(wq_in, 16)
            sp.dma_start(raw_g[:], w_g).then_inc(wq_in, 16)
            sp.dma_start(win_s[:], w_in[0]).then_inc(exp_in, 16)
            sp.dma_start(wout_s[:], w_out[0]).then_inc(exp_in, 16)
            with sp.Fori(1, E) as e:
                sp.wait_ge(me_ready, e * 2)
                sp.dma_start(win_s[:], w_in[bass.ds(e, 1)].rearrange("e p j d -> p (e j) d")).then_inc(exp_in, 16)
                sp.dma_start(wout_s[:], w_out[bass.ds(e, 1)].rearrange("e p j d -> p (e j) d")).then_inc(exp_in, 16)

            def store(n, token_of):
                for j in range(2):
                    sp.wait_ge(sum_ready, n * 2 + (j + 1))
                    for u in range(2):
                        src = hid[B * u:B * u + B, bass.ds(n * 2 + j, 1), :].rearrange("b o d -> b (o d)")
                        sp.dma_start(out[:, token_of(j, u), :].rearrange("b o d -> b (o d)"), src
                                     ).then_inc(out_done, 16)

            with sp.Fori(0, PATCH_PAIRS) as n:
                store(n, lambda j, u: bass.ds(n * 4 + (2 * j + u + 1), 1))
            store(PATCH_PAIRS, lambda j, u: [slice(0, 1), slice(NPATCH + 1, NPATCH + 2)][u] if j == 0
                  else slice(2 * PATCH_TILES + 2 + u, 2 * PATCH_TILES + 3 + u))
            with sp.Fori(PATCH_PAIRS + 1, PAIRS) as n:
                store(n, lambda j, u: bass.ds(n * 4 + (2 * j + u), 1))
            sp.wait_ge(sum_ready, TILES)
            sp.dma_start(out[:, S - 1, :], hid[0:B, LAST, :]).then_inc(out_done, 16)
            sp.wait_ge(out_done, 16 * S)

        @block.tensor
        def _(pe):
            mm = nc.tensor.matmul

            def mm3(dst, l_hi, l_lo, r_hi, r_lo, start, stop):
                mm(dst, l_hi, r_hi, start=start, stop=False)
                mm(dst, l_lo, r_hi, start=False, stop=False)
                return mm(dst, l_hi, r_lo, start=False, stop=stop)

            def position(tile):
                if isinstance(tile, int):
                    return posb_s[:, tile, :]
                return posb_s[:, bass.ds(tile, 1), :].rearrange("p o d -> p (o d)")

            def embed(n, slot):
                after(pe, emb_read, n - (PB - 1))
                for j in range(2):
                    dst = embed_bank(slot)[:, j, :]
                    mm(dst, sel_s[:, 0, :], position(n * 2 + j), start=True, stop=False)
                    for c in range(KP):
                        last = mm(dst, xs[:, 2 * slot + j, c, :], wp[:, c, :], start=False, stop=c == KP - 1)
                last.then_inc(emb_ready, 1)

            def turn(n, slot, rows=(P, P)):
                pe.wait_ge(normed_ready, n + 1)
                after(pe, feat_ready, n - (PB - 1) if slot is not None else n)
                for j, r in enumerate(rows):
                    for c in range(DC):
                        last = nc.tensor.transpose(turned_bank(slot or 0)[:, c, j, 0:r],
                                                   normed[0:r, j, c * P:(c + 1) * P], ident[0:r, 0:r])
                last.then_inc(normed_used, 1)

            pe.wait_ge(w_in_sem, 48)
            pe.wait_ge(c_in, 80)
            for n in range(PB):
                pe.wait_ge(x_in[n], 16)
                embed(n, n)
                if n:
                    turn(n - 1, n - 1)
            with pe.Fori(1, ROUNDS) as r:
                for n in range(PB):
                    pe.wait_ge(x_in[n], r * 16 + 16)
                    embed(r * PB + n, n)
                    turn(r * PB + (n - 1), (n - 1) % PB)
            after(pe, emb_read, PATCH_PAIRS - PB + 1)
            mm(embed_bank(0)[:, 0, :], sel_s[:, 1, :], position(PATCH_TILES), start=True, stop=True
               ).then_inc(emb_ready, 1)
            turn(PATCH_PAIRS - 1, PB - 1)
            with pe.Fori(PATCH_PAIRS, PAIRS) as n:
                turn(n, None)
            turn(PAIRS, None, rows=(B,))

            def project(g, m):
                if m == 0:
                    pe.wait_ge(xs_lo, g + 1)
                for c in range(DC):
                    w = slice(m * P, (m + 1) * P)
                    last = mm3(M[:, 0:GT], wqkv_hi[:, c, w], wqkv_lo[:, c, w], xg_hi[:, c, :], xg_lo[:, c, :],
                               c == 0, c == DC - 1)
                last.then_inc(proj_ready, 1)

            def turn_v(g, half):
                pe.wait_ge(vt_ready, g * 2 + 2)
                for s in range(2):
                    for c in range(DC):
                        t0 = (2 * half + s) * S
                        last = nc.tensor.transpose(M[0:S, s * D + c * P:s * D + (c + 1) * P], vt[:, c, t0:t0 + S],
                                                   ident[:])
                last.then_inc(proj_ready, 1)

            def misc(g, step):
                if step < 3 * DC:
                    project(g, step)
                else:
                    turn_v(g, step - 3 * DC)

            def scores(par, step, s):
                c, sample = step % DC, step // DC
                pe.wait_ge(kbd_ready, s + 1)
                after(pe, probs_ready, s - 1)
                for quad in range(HC // QUAD):
                    dst = psum[0:S, 2 * c + quad, 0:QUAD * SP1]
                    lhs = slice(sample * S, (sample + 1) * S)
                    hs = slice(quad * QUAD, (quad + 1) * QUAD)
                    b0 = (c * HC + quad * QUAD) * SP1
                    mm(dst, bias_l[:], bias_r[:, b0:b0 + QUAD * SP1], start=True, stop=False)
                    last = mm3(dst, qt_hi[:, par, c, lhs], qt_lo[:, par, c, lhs],
                               kbd_hi[:, c, hs, :].rearrange("p h k -> p (h k)"),
                               kbd_lo[:, c, hs, :].rearrange("p h k -> p (h k)"), False, True)
                last.then_inc(s_ready, 1)

            def turn_probs(step, s):
                c = step % DC
                pe.wait_ge(probs_ready, s + 1)
                after(pe, pt_lo_done, s)
                for h in range(HC):
                    q0 = (h % QUAD) * SP1
                    last = nc.tensor.transpose(psum[0:S, PT_BANK + h // QUAD, q0:q0 + S],
                                               probs[:, c, h * SP1:h * SP1 + S], ident[0:S, 0:S])
                last.then_inc(pt_ready, 1)

            def weigh(par, step, s):
                c, sample = step % DC, step // DC
                pe.wait_ge(pt_lo_done, s + 1)
                after(pe, o_read, s)
                for h in range(HC):
                    dst = psum[0:S, O_BANK, h * VW:(h + 1) * VW]
                    rhs = v2[:, par, sample, c * HC + h, :]
                    mm(dst, pt_hi[:, c, h, 0:S], rhs, start=True, stop=False)
                    last = mm(dst, pt_lo[:, c, h, 0:S], rhs, start=False, stop=True)
                last.then_inc(pv_ready, 1)

            def turn_out(sample):
                pe.wait_ge(on_ready, sample * 2 + 2)
                for c in range(DC):
                    last = nc.tensor.transpose(M[:, c * S:(c + 1) * S], o_nat[:, c * P:(c + 1) * P], ident[0:S, 0:S])
                last.then_inc(ot_ready, 1)

            def expert(e, mc):
                pe.wait_ge(exp_in, e * 32 + 32)
                for j in range(JC):
                    last = mm(M[:, 0:D], win_s[:, j, mc * P:(mc + 1) * P], wout_s[:, j, :],
                              start=j == 0, stop=j == JC - 1)
                last.then_inc(me_ready, 1)

            def group(g, par, e, last_group=False):
                for step in range(STEPS):
                    s = g * STEPS + step
                    nxt = (step + 1) % STEPS
                    if not (last_group and step == STEPS - 1):
                        if nxt == 0:
                            pe.wait_ge(q_ready, g * DC + 2 * DC)
                        scores(par if nxt else 1 - par, nxt, s + 1)
                    turn_probs(step, s)
                    if step % 2 and not (isinstance(g, int) and g == 0 and step == 1):
                        last_bank_free(pe, g, "out", step, last_group)
                        turn_out(g * GS + (step // 2 - 1))
                    if step == 2:
                        last_bank_free(pe, g, "expert", step, last_group)
                        expert(e, par)
                    if not (isinstance(g, int) and g == 0 and step == 0):
                        weigh(par if step else 1 - par, (step - 1) % STEPS, s - 1)
                    if not last_group:
                        last_bank_free(pe, g, "proj", step)
                        misc(g + 1, step)
                    if step == 0:
                        pe.wait_ge(v_ready, g * 2 + 2)

            pe.wait_ge(feat_ready, PAIRS + 1)
            pe.wait_ge(w_lo_ready, 3)
            pe.wait_ge(pads_ready, 3)
            for step in range(STEPS):
                if step:
                    projected(pe, 0, step - 1)
                misc(0, step)
            pe.wait_ge(q_ready, DC)
            scores(0, 0, 0)
            group(0, 0, 0)
            group_pairs(pe, group)
            group(GROUPS - 1, 1, E - 1, last_group=True)
            weigh(1, STEPS - 1, GROUPS * STEPS - 1)
            last_bank_free(pe, GROUPS - 1, None, None, True)
            turn_out(B - 1)

            pe.wait_ge(ot_done, B)
            pe.wait_ge(me_done, GROUPS)

            def out_projection(i, j, rows=P):
                pe.wait_ge(of_lo, i + 1)
                after(pe, mid_ready, i)
                for c in range(DC):
                    last = mm3(psum[0:rows, 4, 0:D], of_h[:, j, c, 0:rows], of_l[:, j, c, 0:rows],
                               wo_hi[:, c, :], wo_lo[:, c, :], c == 0, c == DC - 1)
                last.then_inc(wo_ready, 1)

            def turn_mid(i, j, rows=P):
                pe.wait_ge(n2_ready, i + 1)
                after(pe, x2_lo, i)
                for c in range(DC):
                    last = nc.tensor.transpose(psum[:, 5, c * P:c * P + rows], normed[0:rows, j, c * P:(c + 1) * P],
                                               ident[0:rows, 0:rows])
                last.then_inc(x2t_ready, 1)

            def gate(i, j, rows=P):
                pe.wait_ge(x2_lo, i + 1)
                after(pe, g_read, i)
                for c in range(DC):
                    last = mm3(psum[0:rows, 6, 0:E], x2_h[:, j, c, 0:rows], x2_l[:, j, c, 0:rows],
                               wg_hi[:, c, :], wg_lo[:, c, :], c == 0, c == DC - 1)
                last.then_inc(g_ready, 1)

            def experts(i, j, e2, rows=P):
                if 2 * e2 < DVE_E:
                    after(pe, moe_read, i * DVE_E + (2 * e2 + 2 - DVE_E))
                else:
                    after(pe, scaled_ready, i * (E - DVE_E) + (2 * e2 + 2 - E))
                for c in range(DC):
                    last = mm3(psum[0:rows, e2, :], x2_h[:, j, c, 0:rows], x2_l[:, j, c, 0:rows],
                               me_hi[:, c, 2 * e2:2 * e2 + 2, :].rearrange("p e d -> p (e d)"),
                               me_lo[:, c, 2 * e2:2 * e2 + 2, :].rearrange("p e d -> p (e d)"),
                               c == 0, c == DC - 1)
                last.then_inc(moe_ready, 1)

            def tile3(i, j, rows=P, rows1=P, rows2=P):
                experts(i, j, 0, rows)
                experts(i, j, 1, rows)
                if rows1:
                    turn_mid(i + 1, 1 - j, rows1)
                experts(i, j, 2, rows)
                if rows1:
                    gate(i + 1, 1 - j, rows1)
                if rows2:
                    out_projection(i + 2, j, rows2)
                experts(i, j, 3, rows)

            def pair3(n, columns):
                last_pair = isinstance(n, int) and n == PAIRS - 1
                tile3(n * 2, 0, rows2=B if last_pair else P)
                tile3(n * 2 + 1, 1, rows1=B if last_pair else P, rows2=0 if last_pair else P)

            out_projection(0, 0)
            out_projection(1, 1)
            turn_mid(0, 0)
            gate(0, 0)
            pairs(pe, pair3)
            tile3(LAST, 0, rows=B, rows1=0, rows2=0)

        @block.scalar
        def _(act):
            nc.scalar.preload_act_table_set("natural_log_exp_and_others")

            def copy(dst, src, scale=1.0):
                return nc.scalar.activation(dst, src, ACT.Copy, scale=scale)

            def guess(n, j=0, width=2, rows=P):
                act.wait_ge(var_ready, n + 1)
                v, lg, g = (root[0:rows, k, j:j + width] for k in range(3))
                nc.scalar.activation(lg, v, ACT.Ln).then_inc(log_ready, 1)
                act.wait_ge(log_ready, n + 1)
                nc.scalar.activation(g, lg, ACT.Exp, scale=-0.5).then_inc(guess_ready, 1)

            def embedded(n, slot):
                act.wait_ge(emb_ready, n + 1)
                copy(hid[:, bass.ds(n * 2, 2), :], embed_bank(slot)).then_inc(emb_read, 1)

            def turned(n, slot, dst):
                act.wait_ge(normed_used, n + 1)
                copy(dst, turned_bank(slot).rearrange("p c j (t b) -> p c (j t) b", b=B)).then_inc(feat_ready, 1)

            def patch_columns(n):
                return feat_tb[:, :, bass.ds(n * 4 + 1, 4), :]

            for n in range(PB):
                embedded(n, n)
                guess(n)
                if n:
                    turned(n - 1, n - 1, patch_columns(n - 1))
            with act.Fori(1, ROUNDS) as r:
                for n in range(PB):
                    embedded(r * PB + n, n)
                    turned(r * PB + (n - 1), (n - 1) % PB, patch_columns(r * PB + (n - 1)))
                    guess(r * PB + n)
            turned(PATCH_PAIRS - 1, PB - 1, patch_columns(PATCH_PAIRS - 1))
            act.wait_ge(wq_in, 48)
            for dst, src in ((wqkv_hi, raw_qkv), (wo_hi, raw_o), (wg_hi, raw_g)):
                copy(dst[:], src[:]).then_inc(w_hi_ready, 1)
            guess(PATCH_PAIRS)
            act.wait_ge(normed_used, PATCH_PAIRS + 1)
            copy(feat_tb[:, :, 0:NPATCH + 2:NPATCH + 1, :],
                 turned_bank(0)[:, :, 0, :].rearrange("p c (t b) -> p c t b", b=B))
            copy(feat_tb[:, :, NPATCH + 2:NPATCH + 4, :],
                 turned_bank(0)[:, :, 1, :].rearrange("p c (t b) -> p c t b", b=B)).then_inc(feat_ready, 1)
            with act.Fori(PATCH_PAIRS + 1, PAIRS) as n:
                guess(n)
                turned(n, 0, feat_tb[:, :, bass.ds(n * 4, 4), :])
            guess(PAIRS, width=1, rows=B)
            act.wait_ge(normed_used, PAIRS + 1)
            copy(feat_tb[:, :, S - 1, :], turned_bank(0)[:, :, 0, 0:B]).then_inc(feat_ready, 1)

            def misc(g, par, step):
                if step < 2 * DC:
                    act.wait_ge(proj_ready, g * STEPS + (step + 1))
                    if step < DC:
                        copy(qt_hi[:, par, step, :], M[:, 0:GT], HD ** -0.5).then_inc(proj_hi, 1)
                    else:
                        copy(kt_hi[:, par, step - DC, :, 0:S], M[:, 0:GT].rearrange("p (s t) -> p s t", s=GS)).then_inc(proj_hi, 1)
                elif step < 3 * DC:
                    act.wait_ge(proj_ready, g * STEPS + (step + 1))
                    copy(vt[:, step - 2 * DC, :], M[:, 0:GT]).then_inc(vt_ready, 1)
                else:
                    act.wait_ge(proj_ready, g * STEPS + (step + 1))
                    half = step - 3 * DC
                    copy(v2[:, par, 2 * half:2 * half + 2, :, 0:HD],
                         M[0:S, :].rearrange("p (s h d) -> p s h d", s=2, h=H)).then_inc(proj_hi, 1)

            def exponentials(step, s):
                c = step % DC
                act.wait_ge(max_done, s + 1)
                after(act, pt_ready, s - 1)
                for h in range(QUAD):
                    nc.scalar.activation(probs[:, c, (QUAD + h) * SP1:(QUAD + h) * SP1 + S],
                                         psum[0:S, 2 * c + 1, h * SP1:h * SP1 + S], ACT.Exp,
                                         bias=rowmax[:, c, QUAD + h:QUAD + h + 1])
                act.wait_ge(shifted_ready, s + 1)
                quad = probs[:, c, 0:QUAD * SP1]
                nc.scalar.activation(quad, quad, ACT.Exp).then_inc(probs_ready, 1)

            def probs_hi(step, s):
                c = step % DC
                act.wait_ge(pt_ready, s + 1)
                after(act, pv_ready, s - 1)
                copy(pt_hi[:, c, :, 0:S].rearrange("p (b h) q -> p b h q", b=2), pt_banks()).then_inc(pt_hi_done, 1)

            def out_low(s):
                act.wait_ge(pv_ready, s + 1)
                after(act, o_read, s)
                copy(otmp[:], o_bank()[:, :, HD:2 * HD]).then_inc(otmp_ready, 1)

            def out_turned(sample):
                act.wait_ge(ot_ready, sample + 1)
                copy(sample_columns(sample), M[:, 0:DC * S].rearrange("p (c t) -> p c t", c=DC)
                     ).then_inc(ot_done, 1)

            def expert(g, e, par):
                act.wait_ge(me_ready, g + 1)
                copy(me_slice(me_hi, e, par), M[:, 0:D]).then_inc(me_hi_done, 1)

            def group(g, par, e, last_group=False):
                for step in range(STEPS):
                    s = g * STEPS + step
                    probs_hi(step, s)
                    if step % 2 and not (isinstance(g, int) and g == 0 and step == 1):
                        out_turned(g * GS + (step // 2 - 1))
                    if not (last_group and step == STEPS - 1):
                        exponentials((step + 1) % STEPS, s + 1)
                    if step == 2:
                        expert(g, e, par)
                    if not (isinstance(g, int) and g == 0 and step == 0):
                        out_low(s - 1)
                    if not last_group:
                        misc(g + 1, 1 - par, step)

            act.wait_ge(feat_ready, PAIRS + 1)
            act.wait_ge(w_lo_ready, 3)
            act.wait_ge(pads_ready, 3)
            for step in range(STEPS):
                misc(0, 0, step)
            exponentials(0, 0)
            group(0, 0, 0)
            group_pairs(act, group)
            group(GROUPS - 1, 1, E - 1, last_group=True)
            out_low(GROUPS * STEPS - 1)
            out_turned(B - 1)

            def spread(i, j, src):
                after(act, wo_ready, i - 1)
                copy(of_h[:, j].rearrange("p c (t b) -> p c t b", b=B)[:, :, 0:src.shape[2], :], src
                     ).then_inc(of_hi, 1)

            def mid_hi(i, j, rows=P):
                act.wait_ge(x2t_ready, i + 1)
                after(act, moe_ready, i * 4 - 4)
                copy(x2_h[:, j, :, 0:rows], psum[:, 5, 0:D].rearrange("p (c r) -> p c r", c=DC)[:, :, 0:rows]
                     ).then_inc(x2_hi, 1)

            def gate_exp(i, rows=P):
                act.wait_ge(gd_ready, i + 1)
                nc.scalar.activation(gtmp[0:rows, 2, 1:2], gtmp[0:rows, 2, 0:1], ACT.Exp).then_inc(ge_ready, 1)

            def scale(i, j, e2, rows=P):
                act.wait_ge(moe_ready, i * 4 + (e2 + 1))
                act.wait_ge(gates_ready, i + 1)
                for e in (2 * e2, 2 * e2 + 1):
                    after(act, part_ready, i * 3 - (0 if e == E - 1 else 1 if e == E - 2 else 2))
                    nc.scalar.activation(scaled[0:rows, e - DVE_E, :],
                                         psum[0:rows, e2, (e % 2) * D:(e % 2 + 1) * D], ACT.Copy,
                                         scale=gtmp[0:rows, 6 + j, e:e + 1]).then_inc(scaled_ready, 1)

            def tile3(i, j, rows=P, rows1=P, rows2=P, ahead=None):
                if ahead is not None:
                    spread(i + 2, j, ahead)
                if rows1:
                    mid_hi(i + 1, 1 - j, rows1)
                scale(i, j, 2, rows)
                if rows1:
                    gate_exp(i + 1, rows1)
                if rows2:
                    guess(i + (PAIRS + 3), j, 1, rows2)
                scale(i, j, 3, rows)

            def pair3(n, columns):
                last_pair = isinstance(n, int) and n == PAIRS - 1
                tile3(n * 2, 0, rows2=B if last_pair else P, ahead=columns(feat_tb, 0))
                tile3(n * 2 + 1, 1, rows1=B if last_pair else P, rows2=0 if last_pair else P,
                      ahead=None if last_pair else columns(feat_tb, 1))

            act.wait_ge(me_done, GROUPS)
            act.wait_ge(ot_done, B)
            for j in range(2):
                spread(j, j, token_columns(feat_tb, 0, j))
            guess(PAIRS + 1, 0, 1)
            mid_hi(0, 0)
            gate_exp(0)
            guess(PAIRS + 2, 1, 1)
            pairs(act, pair3)
            tile3(LAST, 0, rows=B, rows1=0, rows2=0)

        @block.gpsimd
        def _(pool):
            pool.wait_ge(feat_ready, PAIRS + 1)
            pool.wait_ge(w_lo_ready, 3)
            nc.gpsimd.memset(kt_hi[:, :, :, :, S:SP1].bitcast(F32), 0.0).then_inc(pads_ready, 1)
            nc.gpsimd.memset(kt_lo[:, :, :, :, S:SP1].bitcast(F32), 0.0).then_inc(pads_ready, 1)
            nc.gpsimd.memset(v2[:, :, :, :, 2 * HD:VW].bitcast(F32), 1.0).then_inc(pads_ready, 1)
            pool.wait_ge(pads_ready, 3)
            pool.wait_ge(c_in, 80)

            def spread_keys(g, par, step, s):
                c, sample = step % DC, step // DC
                if sample == 0:
                    pool.wait_ge(k_ready, g * DC + DC)
                after(pool, s_ready, s - 1)
                mask = head_mask[:].rearrange("p (h o) -> p h o", o=1).to_broadcast([P, HC, SP1])
                for dst, src in ((kbd_hi, kt_hi), (kbd_lo, kt_lo)):
                    k = src[:, par, c, sample, :].rearrange("p (o k) -> p o k", o=1).to_broadcast([P, HC, SP1])
                    last = nc.gpsimd.tensor_tensor(out=dst[:, c], in0=k, in1=mask, op=ALU.mult)
                last.then_inc(kbd_ready, 1)

            def split_hi(g):
                after(pool, proj_ready, g * STEPS + (3 * DC - STEPS))
                nc.gpsimd.tensor_copy(xg_hi[:], group_columns(g)).then_inc(xs_hi, 1)

            def split_lo(g):
                nc.gpsimd.tensor_tensor(out=xg_lo[:], in0=group_columns(g), in1=xg_hi[:], op=ALU.subtract
                                        ).then_inc(xs_lo, 1)

            def group(g, par, e, last_group=False):
                for step in range(STEPS):
                    later = (step + 2) % STEPS
                    s = g * STEPS + step + 2
                    splits = step == 0 and not last_group
                    if splits:
                        split_hi(g + 1)
                        pool.wait_ge(xs_hi, g + 2)
                    if step + 2 < STEPS:
                        spread_keys(g, par, later, s)
                    elif not last_group:
                        spread_keys(g + 1, 1 - par, later, s)
                    if splits:
                        split_lo(g + 1)

            split_hi(0)
            pool.wait_ge(xs_hi, 1)
            split_lo(0)
            spread_keys(0, 0, 0, 0)
            spread_keys(0, 0, 1, 1)
            group(0, 0, 0)
            group_pairs(pool, group)
            group(GROUPS - 1, 1, E - 1, last_group=True)

            def spread(i, j, src):
                pool.wait_ge(of_hi, i + 1)
                r = src.shape[2]
                nc.gpsimd.tensor_tensor(out=of_l[:, j].rearrange("p c (t b) -> p c t b", b=B)[:, :, 0:r, :], in0=src,
                                        in1=of_h[:, j].rearrange("p c (t b) -> p c t b", b=B)[:, :, 0:r, :],
                                        op=ALU.subtract).then_inc(of_lo, 1)

            def total(i, tile, rows=P):
                p, q = part[0:rows, 0, :], part[0:rows, 1, :]
                pool.wait_ge(scaled_ready, i * (E - DVE_E) + 2)
                after(pool, sum_ready, i)
                nc.gpsimd.tensor_tensor(out=p, in0=scaled[0:rows, 0, :], in1=scaled[0:rows, 1, :], op=ALU.add
                                        ).then_inc(part_ready, 1)
                pool.wait_ge(scaled_ready, i * (E - DVE_E) + 4)
                nc.gpsimd.tensor_tensor(out=q, in0=scaled[0:rows, 2, :], in1=scaled[0:rows, 3, :], op=ALU.add
                                        ).then_inc(part_ready, 1)
                pool.wait_ge(part_ready, i * 3 + 2)
                nc.gpsimd.tensor_tensor(out=p, in0=p, in1=q, op=ALU.add).then_inc(part_ready, 1)
                pool.wait_ge(part_ready, i * 3 + 3)
                pool.wait_ge(moe_read, i * DVE_E + DVE_E)
                nc.gpsimd.tensor_tensor(out=tile, in0=p, in1=tile, op=ALU.add).then_inc(sum_ready, 1)

            def pair3(n, columns):
                last_pair = isinstance(n, int) and n == PAIRS - 1
                for j in range(2):
                    if not (last_pair and j):
                        spread(n * 2 + (2 + j), j, columns(feat_tb, j))
                    total(n * 2 + j, hid_tile(n, j))

            for j in range(2):
                spread(j, j, token_columns(feat_tb, 0, j))
            pairs(pool, pair3)
            total(LAST, hid_tile(PAIRS, 0, B), B)

        @block.vector
        def _(dve):
            tt = nc.vector.tensor_tensor

            def moments(stats_ready, count, total, tiles):
                for j, r, source in tiles:
                    last = nc.vector.bn_stats(stats[0:r, j, :], source)
                last.then_inc(stats_ready, 1)
                dve.wait_ge(c_in, 80)
                dve.wait_ge(stats_ready, count)
                for j, r, source in tiles:
                    last = nc.vector.bn_aggr(mv[0:r, j, :], stats[0:r, j, :])
                last.then_inc(aggr_ready, 1)
                dve.wait_ge(aggr_ready, total + 1)
                j0, r = tiles[0][0], tiles[0][1]
                nc.vector.tensor_scalar_add(root[0:r, 0, j0:j0 + len(tiles)], mv[0:r, j0:j0 + len(tiles), 1], EPS
                                            ).then_inc(var_ready, 1)

            def normalised(chain, count, tiles, used, done):
                j0, r, w = tiles[0][0], tiles[0][1], len(tiles)
                v, g = root[0:r, 0, j0:j0 + w], root[0:r, 2, j0:j0 + w]
                rs = rstd[0:r, j0:j0 + w]
                dve.wait_ge(guess_ready, count + 1)
                tt(out=rs, in0=g, in1=g, op=ALU.mult).then_inc(dve_chain, 1)
                dve.wait_ge(dve_chain, chain + 1)
                nc.vector.scalar_tensor_tensor(out=rs, in0=rs, scalar=-0.5, in1=v, op0=ALU.mult, op1=ALU.mult
                                               ).then_inc(dve_chain, 1)
                dve.wait_ge(dve_chain, chain + 2)
                nc.vector.scalar_tensor_tensor(out=rs, in0=rs, scalar=1.5, in1=g, op0=ALU.add, op1=ALU.mult
                                               ).then_inc(dve_chain, 1)
                dve.wait_ge(dve_chain, chain + 3)
                used()
                for j, r, source in tiles:
                    last = nc.vector.tensor_scalar(normed[0:r, j, :], source, mv[0:r, j, 0:1], rstd[0:r, j:j + 1],
                                                   ALU.subtract, ALU.mult)
                last.then_inc(done, 1)

            def norm1(n, wait_source, rows=(P, P), done=None):
                tiles = [(j, r, hid_tile(n, j, r)) for j, r in enumerate(rows)]
                wait_source()
                moments(stats1, n + 1 if done is None else done, n, tiles)
                normalised(n * 3, n, tiles, lambda: after(dve, normed_used, n), normed_ready)

            def class_rows():
                dve.wait_ge(emb_ready, PATCH_PAIRS + 1)
                tt(out=hid_tile(PATCH_PAIRS, 0, B), in0=embed_bank(0)[0:B, 0, :], in1=hid_tile(PATCH_PAIRS, 0, B),
                   op=ALU.add).then_inc(emb_read, 1)

            def split_weights():
                dve.wait_ge(w_hi_ready, 3)
                for lo, raw, hi in ((wqkv_lo, raw_qkv, wqkv_hi), (wo_lo, raw_o, wo_hi), (wg_lo, raw_g, wg_hi)):
                    tt(out=lo[:], in0=raw[:], in1=hi[:], op=ALU.subtract).then_inc(w_lo_ready, 1)

            norm1(0, lambda: dve.wait_ge(emb_read, 1))
            with dve.Fori(1, PATCH_PAIRS) as n:
                norm1(n, lambda: dve.wait_ge(emb_read, n + 1))
            dve.wait_ge(base_in, 32)
            class_rows()
            dve.wait_ge(emb_read, PATCH_PAIRS + 1)
            with dve.Fori(PATCH_PAIRS + 1, PAIRS + 1) as done:
                norm1(done - 1, lambda: None, done=done)
            norm1(PAIRS, lambda: None, rows=(B,))
            split_weights()

            def misc(g, par, step):
                if step < DC:
                    dve.wait_ge(proj_hi, g * 6 + (step + 1))
                    nc.vector.scalar_tensor_tensor(out=qt_lo[:, par, step, :], in0=M[:, 0:GT], scalar=HD ** -0.5,
                                                   in1=qt_hi[:, par, step, :], op0=ALU.mult, op1=ALU.subtract
                                                   ).then_inc(q_ready, 1)
                    return "q"
                if step < 2 * DC:
                    dve.wait_ge(proj_hi, g * 6 + (step + 1))
                    tt(out=kt_lo[:, par, step - DC, :, 0:S], in0=M[:, 0:GT].rearrange("p (s t) -> p s t", s=GS),
                       in1=kt_hi[:, par, step - DC, :, 0:S], op=ALU.subtract).then_inc(k_ready, 1)
                elif step >= 3 * DC:
                    half = step - 3 * DC
                    dve.wait_ge(proj_hi, g * 6 + (2 * DC + half + 1))
                    tt(out=v2[:, par, 2 * half:2 * half + 2, :, HD:2 * HD],
                       in0=M[0:S, :].rearrange("p (s h d) -> p s h d", s=2, h=H),
                       in1=v2[:, par, 2 * half:2 * half + 2, :, 0:HD], op=ALU.subtract).then_inc(v_ready, 1)

            def row_maxima(step, s):
                c = step % DC
                dve.wait_ge(s_ready, s + 1)
                sc = psum[0:S, 2 * c:2 * c + 2, 0:QUAD * SP1].rearrange("p b (h k) -> p b h k", k=SP1)
                mx = rowmax[:, c, :].rearrange("p (b h) -> p b h", b=2)
                after(dve, probs_ready, s - 1)
                nc.vector.tensor_reduce(out=mx, in_=sc[:, :, :, 0:S], op=ALU.max, axis=AX_X, negate=True
                                        ).then_inc(max_done, 1)
                dve.wait_ge(max_done, s + 1)
                after(dve, pt_ready, s - 1)
                tt(out=probs[:, c, 0:QUAD * SP1].rearrange("p (h k) -> p h k", k=SP1), in0=sc[:, 0],
                   in1=mx[:, 0].rearrange("p (h o) -> p h o", o=1).to_broadcast([S, QUAD, SP1]), op=ALU.add
                   ).then_inc(shifted_ready, 1)

            def probs_lo(step, s):
                c = step % DC
                dve.wait_ge(pt_hi_done, s + 1)
                tt(out=pt_lo[:, c, :, 0:S].rearrange("p (b h) q -> p b h q", b=2), in0=pt_banks(),
                   in1=pt_hi[:, c, :, 0:S].rearrange("p (b h) q -> p b h q", b=2), op=ALU.subtract
                   ).then_inc(pt_lo_done, 1)

            def normalise(step, s, sample_turned):
                c = step % DC
                dve.wait_ge(otmp_ready, s + 1)
                after(dve, on_ready, s)
                nc.vector.reciprocal(rden[:, c, :], o_bank()[:, :, 2 * HD])
                tt(out=osum[:], in0=o_bank()[:, :, 0:HD], in1=otmp[:], op=ALU.add).then_inc(o_read, 1)
                dve.wait_ge(o_read, s + 1)
                if sample_turned is not None:
                    after(dve, ot_ready, sample_turned)
                tt(out=o_nat[:, c * P:(c + 1) * P].rearrange("p (h d) -> p h d", h=HC), in0=osum[:],
                   in1=rden[:, c, :].rearrange("p (h o) -> p h o", o=1).to_broadcast([S, HC, HD]), op=ALU.mult
                   ).then_inc(on_ready, 1)

            def expert(g, e, par):
                dve.wait_ge(me_hi_done, g + 1)
                tt(out=me_slice(me_lo, e, par), in0=M[:, 0:D], in1=me_slice(me_hi, e, par), op=ALU.subtract
                   ).then_inc(me_done, 1)

            def group(g, par, e, last_group=False):
                for step in range(STEPS):
                    s = g * STEPS + step
                    if not (last_group and step == STEPS - 1):
                        row_maxima((step + 1) % STEPS, s + 1)
                    probs_lo(step, s)
                    if step == 2:
                        expert(g, e, par)
                    if not (isinstance(g, int) and g == 0 and step == 0):
                        normalise((step - 1) % STEPS, s - 1, g * GS + (step - 1) // 2)
                    if not last_group:
                        misc(g + 1, 1 - par, step)

            for step in range(STEPS):
                misc(0, 0, step)
            row_maxima(0, 0)
            group(0, 0, 0)
            group_pairs(dve, group)
            group(GROUPS - 1, 1, E - 1, last_group=True)
            normalise(STEPS - 1, GROUPS * STEPS - 1, B - 1)

            base_chain = 3 * (PAIRS + 1)

            def middle(i, j, tile, rows=P):
                dve.wait_ge(wo_ready, i + 1)
                tt(out=tile, in0=psum[0:rows, 4, 0:D], in1=tile, op=ALU.add).then_inc(mid_ready, 1)
                dve.wait_ge(c_in, 80)
                dve.wait_ge(mid_ready, i + 1)
                moments(stats3, i + 1, i + (PAIRS + 1), [(j, rows, tile)])

            def norm2(i, j, tile, rows=P):
                normalised(i * CH + base_chain, i + (PAIRS + 1), [(j, rows, tile)], lambda: None, n2_ready)

            CH = 9

            def mid_lo(i, j, rows=P):
                dve.wait_ge(x2_hi, i + 1)
                view = psum[:, 5, 0:D].rearrange("p (c r) -> p c r", c=DC)[:, :, 0:rows]
                tt(out=x2_l[:, j, :, 0:rows], in0=view, in1=x2_h[:, j, :, 0:rows], op=ALU.subtract
                   ).then_inc(x2_lo, 1)

            def gates(i, j, rows=P):
                r = slice(0, rows)
                chain = i * CH + base_chain
                n = [3]

                def link(ins):
                    n[0] += 1
                    ins.then_inc(dve_chain, 1)
                    dve.wait_ge(dve_chain, chain + n[0])

                dve.wait_ge(g_ready, i + 1)
                nc.vector.tensor_copy(gtmp[r, 0, :], psum[r, 6, 0:E]).then_inc(g_read, 1)
                dve.wait_ge(c_in, 80)
                dve.wait_ge(g_read, i + 1)
                link(nc.vector.max(gtmp[r, 1, :], gtmp[r, 0, :]))
                tt(out=gtmp[r, 2, 0:1], in0=gtmp[r, 1, 1:2], in1=gtmp[r, 1, 0:1], op=ALU.subtract
                   ).then_inc(gd_ready, 1)
                link(nc.vector.max_index(gidx[r, :], gtmp[r, 1, :], gtmp[r, 0, :]))
                nc.vector.tensor_copy(gtmp[r, 3, 0:2], gidx[r, 0:2])
                dve.wait_ge(ge_ready, i + 1)
                link(nc.vector.tensor_scalar_add(gtmp[r, 4, 0:1], gtmp[r, 2, 1:2], 1.0))
                link(nc.vector.reciprocal(gtmp[r, 4, 1:2], gtmp[r, 4, 0:1]))
                tt(out=gtmp[r, 4, 2:3], in0=gtmp[r, 2, 1:2], in1=gtmp[r, 4, 1:2], op=ALU.mult)
                link(nc.vector.tensor_scalar(gtmp[r, 5, :], iota[r, :], gtmp[r, 3, 0:1], gtmp[r, 4, 1:2],
                                             ALU.is_equal, ALU.mult))
                link(nc.vector.tensor_scalar(gtmp[r, 0, :], iota[r, :], gtmp[r, 3, 1:2], gtmp[r, 4, 2:3],
                                             ALU.is_equal, ALU.mult))
                after(dve, scaled_ready, (i - 1) * (E - DVE_E))
                tt(out=gtmp[r, 6 + j, :], in0=gtmp[r, 5, :], in1=gtmp[r, 0, :], op=ALU.add).then_inc(gates_ready, 1)

            def combine(i, j, tile, e2, rows=P):
                dve.wait_ge(moe_ready, i * 4 + (e2 + 1))
                dve.wait_ge(gates_ready, i + 1)
                for e in (2 * e2, 2 * e2 + 1):
                    if e:
                        dve.wait_ge(moe_read, i * DVE_E + e)
                    nc.vector.scalar_tensor_tensor(out=tile, in0=psum[0:rows, e2, (e % 2) * D:(e % 2 + 1) * D],
                                                   scalar=gtmp[0:rows, 6 + j, e:e + 1], in1=tile,
                                                   op0=ALU.mult, op1=ALU.add).then_inc(moe_read, 1)

            def tile3(n, j, rows=P, rows1=P, rows2=P):
                i = n * 2 + j
                tile = hid_tile(n, j, rows)
                combine(i, j, tile, 0, rows)
                if rows1:
                    norm2(i + 1, 1 - j, hid_tile(n + j, 1 - j, rows1), rows1)
                combine(i, j, tile, 1, rows)
                if rows1:
                    mid_lo(i + 1, 1 - j, rows1)
                    gates(i + 1, 1 - j, rows1)
                if rows2:
                    middle(i + 2, j, hid_tile(n + 1, j, rows2), rows2)

            def pair3(n, columns):
                last_pair = isinstance(n, int) and n == PAIRS - 1
                tile3(n, 0, rows2=B if last_pair else P)
                tile3(n, 1, rows1=B if last_pair else P, rows2=0 if last_pair else P)

            dve.wait_ge(ot_done, B)
            middle(0, 0, hid_tile(0, 0))
            norm2(0, 0, hid_tile(0, 0))
            mid_lo(0, 0)
            gates(0, 0)
            middle(1, 1, hid_tile(0, 1))
            pairs(dve, pair3)
            tile3(PAIRS, 0, rows=B, rows1=0, rows2=0)


def constants():
    import numpy as np
    bf = np.dtype("bfloat16")

    def parts(a):
        hi = a.astype(bf)
        mid = (a - hi.astype(np.float32)).astype(bf)
        lo = (a - hi.astype(np.float32) - mid.astype(np.float32)).astype(bf)
        return hi, mid, lo

    slopes = (np.float32(1.0) / np.power(np.float32(256.0), (np.arange(H, dtype=np.float32) + 1) / np.float32(H))
              ).astype(np.float32)
    left = np.zeros((NBIAS, S), bf)
    right = np.zeros((NBIAS, H, SP1), bf)
    left[:S] = np.eye(S)
    q, k = np.arange(S), np.arange(SP1)
    right[:S] = np.where((k[None, :] > q[:, None]) | (k[None, :] >= S), np.float32(-2.0 ** 100), 0)[:, None, :]
    for n, part in enumerate(parts(slopes)):
        left[S + n] = q
        right[S + n] = -part[:, None]
    for n, part in enumerate(parts(slopes[:, None] * k.astype(np.float32)[None, :])):
        left[S + 3 + n] = 1
        right[S + 3 + n] = part
    sel = np.zeros((3, 2, P), np.float32)
    sel[0, :, :B] = 1
    sel[1, :, B:] = 1
    sel[2, 0, :] = 1
    mask = (np.arange(P)[:, None] // HD == np.arange(HC)[None, :]).astype(np.float32)
    iota = np.broadcast_to(np.arange(E, dtype=np.float32), (P, E)).copy()
    return {"sel": sel, "ident": np.eye(P, dtype=np.float32), "bias_l": left, "bias_r": right.reshape(NBIAS, -1),
            "head_mask": mask, "iota": iota}


def kernel(x, txt, L0_tok_W, L0_tok_b, L0_tok_class_token, L0_tok_pos_emb, L0_attn_W_Q, L0_attn_W_K, L0_attn_W_V,
           L0_attn_W_O, L0_ffn_w_gate, L0_ffn_w_in, L0_ffn_w_out):
    import numpy as np
    import concourse.bacc as bacc
    from concourse import mybir as mb
    from concourse.bass_utils import run_bass_kernel_spmd

    x, txt = np.asarray(x), np.asarray(txt)
    n = IMG // PATCH
    pat = x.reshape(B, CIN, n, PATCH, n, PATCH).transpose(1, 3, 5, 2, 4, 0).reshape(KP, P, PATCH_TILES, 2 * B)
    pat = np.ascontiguousarray(pat.transpose(2, 1, 0, 3))
    cls = np.broadcast_to(np.asarray(L0_tok_class_token).reshape(1, 1, D), (1, B, D))
    base = np.concatenate([cls, txt.transpose(1, 0, 2)], axis=0).reshape(-1, D)
    pos = np.asarray(L0_tok_pos_emb).reshape(NPATCH + 1, D)
    rows = np.zeros((2 * TILES, D), pos.dtype)
    rows[:NPATCH], rows[NPATCH] = pos[1:], pos[0]
    bias = np.broadcast_to(np.asarray(L0_tok_b).reshape(1, 1, D), (1, TILES, D))
    posb = np.concatenate([rows.reshape(TILES, 2, D).transpose(1, 0, 2), bias], axis=0)

    def by_row(w):
        return np.ascontiguousarray(w.reshape(-1, P, w.shape[1]).transpose(1, 0, 2))

    wq, wk, wv = (np.asarray(w) for w in (L0_attn_W_Q, L0_attn_W_K, L0_attn_W_V))
    inputs = {
        "x_t": pat, "base": base, "posb": posb,
        "w_patch": by_row(np.asarray(L0_tok_W)),
        "w_qkv": by_row(np.concatenate([wq.T, wk.T, wv.T], axis=1)),
        "w_o": by_row(np.asarray(L0_attn_W_O).T),
        "w_g": by_row(np.asarray(L0_ffn_w_gate).T),
        "w_in": np.asarray(L0_ffn_w_in).reshape(E, P, JC, D),
        "w_out": np.ascontiguousarray(np.asarray(L0_ffn_w_out).transpose(0, 2, 1)).reshape(E, P, JC, D),
    }
    inputs.update(constants())
    order = ["x_t", "base", "posb", "sel", "w_patch", "w_qkv", "w_o", "w_g", "w_in", "w_out", "ident", "bias_l",
             "bias_r", "head_mask", "iota"]
    nc = bacc.Bacc("TRN2", target_bir_lowering=False, num_devices=1)
    arrays, aps = {}, []
    for name in order:
        a = np.ascontiguousarray(inputs[name])
        arrays[f"in_{name}"] = a
        aps.append(nc.dram_tensor(f"in_{name}", a.shape, mb.dt.from_np(a.dtype), kind="ExternalInput").ap())
    out = nc.dram_tensor("out", (B, S, D), F32, kind="ExternalOutput").ap()
    fusion_block(nc, *aps, out)
    r = run_bass_kernel_spmd(nc, [arrays], core_ids=[0])
    return r.results[0]["out"]
```

```python
from contextlib import ExitStack

import concourse.bass as bass
from concourse import mybir

ALU = mybir.AluOpType
ACT = mybir.ActivationFunctionType
AX_X = mybir.AxisListType.X
F32 = mybir.dt.float32
F32R = mybir.dt.float32r
BF16 = mybir.dt.bfloat16
U32 = mybir.dt.uint32

P = 128
B, CIN, IMG, PATCH = 64, 3, 96, 16
NPATCH = (IMG // PATCH) ** 2
TXT = 32
S = 1 + NPATCH + TXT
D, H, E, HID = 256, 16, 8, 1024
HD = D // H
DC = D // P
KP = CIN * PATCH * PATCH // P
JC = HID // P
EPS = 1e-5

TILES = (S + 1) // 2
PATCH_TILES = NPATCH // 2
XSLOT = 6
SP1 = S + 1

HC = H // DC
QUAD = 4
GS = 4
GT = GS * S
GROUPS = B // GS
STEPS = GS * DC
VW = 2 * HD + 2
NBIAS = S + 6
DVE_E = 4


def after(engine, semaphore, value):
    if isinstance(value, int) and value <= 0:
        return
    engine.wait_ge(semaphore, value)


def fusion_block(nc, x_t, base, posb, sel, w_patch, w_qkv, w_o, w_g, w_in, w_out, ident_d, bias_l_d, bias_r_d,
                 head_mask_d, iota_d, out):
    ctx = ExitStack()
    with ctx:
        def sb(name, shape, dt=F32):
            return ctx.enter_context(nc.sbuf_tensor(name, shape, dt))

        def sem(name):
            return ctx.enter_context(nc.semaphore(name))

        hid = sb("hid", [P, TILES, D])
        feat = sb("feat", [P, DC, B, S])
        feat_flat = feat[:].rearrange("p c b t -> p c (b t)")
        feat_tb = feat[:].rearrange("p c b t -> p c t b")
        ident = sb("ident", [P, P])
        wqkv_hi, wqkv_lo = sb("wqkv_hi", [P, DC, 3 * D], F32R), sb("wqkv_lo", [P, DC, 3 * D], F32R)
        wo_hi, wo_lo = sb("wo_hi", [P, DC, D], F32R), sb("wo_lo", [P, DC, D], F32R)
        wg_hi, wg_lo = sb("wg_hi", [P, DC, E], F32R), sb("wg_lo", [P, DC, E], F32R)
        head_mask = sb("head_mask", [P, HC])
        iota = sb("iota", [P, E])
        bias_l = sb("bias_l", [NBIAS, S], BF16)
        bias_r = sb("bias_r", [NBIAS, H * SP1], BF16)
        win_s = sb("win_s", [P, JC, D])
        wout_s = sb("wout_s", [P, JC, D])
        stats = sb("stats", [P, 4, 6])
        mv = sb("mv", [P, 4, 2])
        rstd = sb("rstd", [P, 4])
        root = sb("root", [P, 3, 4])
        normed = sb("normed", [P, 4, D])
        gtmp = sb("gtmp", [P, 8, E])
        gidx = sb("gidx", [P, E], U32)
        psum = ctx.enter_context(nc.psum_tensor("psum", [P, 8, 512], F32))

        w_in_sem = sem("patch_weights_in")
        c_in = sem("constants_in")
        wq_in = sem("attention_weights_in")
        first_base_in, base_in = sem("first_base_in"), sem("base_in")
        class_ready = sem("class_ready")
        x_in = [sem(f"x_in{n}") for n in range(XSLOT // 2)]
        emb_ready, emb_read = sem("emb_ready"), sem("emb_read")
        hid_ready = sem("hid_ready")
        dve_chain = sem("dve_chain")
        stats1, stats3, aggr_ready = sem("stats1_ready"), sem("stats3_ready"), sem("aggr_ready")
        var_ready, log_ready, guess_ready = sem("var_ready"), sem("log_ready"), sem("guess_ready")
        normed_ready, normed_used = sem("normed_ready"), sem("normed_used")
        feat_ready = sem("feat_ready")
        w_hi_ready, w_lo_ready = sem("w_hi_ready"), sem("w_lo_ready")
        pads_ready = sem("pads_ready")

        exp_in = sem("expert_in")
        xs_hi, xs_lo = sem("xs_hi"), sem("xs_lo")
        proj_ready = sem("proj_ready")
        proj_hi = sem("proj_hi")
        q_ready, k_ready, vt_ready, v_ready = sem("q_ready"), sem("k_ready"), sem("vt_ready"), sem("v_ready")
        ot_ready, me_ready, me_hi_done, me_done = sem("ot_ready"), sem("me_ready"), sem("me_hi_done"), sem("me_done")
        ot_done = sem("ot_done")
        kbd_ready = sem("kbd_ready")
        s_ready, max_done, shifted_ready = sem("s_ready"), sem("max_done"), sem("shifted_ready")
        probs_ready, pt_ready, pt_hi_done, pt_lo_done = (sem("probs_ready"), sem("pt_ready"), sem("pt_hi_done"),
                                                         sem("pt_lo_done"))
        pv_ready, otmp_ready, o_read, on_ready = sem("pv_ready"), sem("otmp_ready"), sem("o_read"), sem("on_ready")

        of_hi, of_lo = sem("of_hi"), sem("of_lo")
        wo_ready, mid_ready = sem("wo_ready"), sem("mid_ready")
        n2_ready, x2t_ready, x2_hi, x2_lo = sem("n2_ready"), sem("x2t_ready"), sem("x2_hi_done"), sem("x2_lo_done")
        g_ready, g_read, gd_ready, ge_ready, gates_ready = (sem("g_ready"), sem("g_read"), sem("gd_ready"),
                                                            sem("ge_ready"), sem("gates_ready"))
        moe_ready, moe_read = sem("moe_ready"), sem("moe_read")
        scaled_ready, part_ready, sum_ready = sem("scaled_ready"), sem("part_ready"), sem("sum_ready")
        out_done = sem("out_done")

        early = ExitStack()
        xs = early.enter_context(nc.sbuf_tensor("xs", [P, XSLOT, KP, P], F32))
        wp = early.enter_context(nc.sbuf_tensor("wp", [P, KP, D], F32))
        posb_s = early.enter_context(nc.sbuf_tensor("posb_s", [3, PATCH_TILES + 1, D], F32))
        sel_s = early.enter_context(nc.sbuf_tensor("sel_s", [3, 2, P], F32))
        raw_qkv = early.enter_context(nc.sbuf_tensor("raw_qkv", [P, DC, 3 * D], F32))
        raw_o = early.enter_context(nc.sbuf_tensor("raw_o", [P, DC, D], F32))
        raw_g = early.enter_context(nc.sbuf_tensor("raw_g", [P, DC, E], F32))
        early.close()
        me_hi, me_lo = sb("me_hi", [P, DC, E, D], F32R), sb("me_lo", [P, DC, E, D], F32R)
        late = ExitStack()

        def lsb(name, shape, dt=F32):
            return late.enter_context(nc.sbuf_tensor(name, shape, dt))

        of_h, of_l = lsb("of_h", [P, 2, DC, P], F32R), lsb("of_l", [P, 2, DC, P], F32R)
        x2_h, x2_l = lsb("x2_h", [P, 2, DC, P], F32R), lsb("x2_l", [P, 2, DC, P], F32R)
        scaled = lsb("scaled", [P, E - DVE_E, D])
        part = lsb("part", [P, 2, D])
        late.close()
        mid = ExitStack()

        def msb(name, shape, dt=F32):
            return mid.enter_context(nc.sbuf_tensor(name, shape, dt))

        xg_hi, xg_lo = msb("xg_hi", [P, DC, GT], F32R), msb("xg_lo", [P, DC, GT], F32R)
        qt_hi, qt_lo = msb("qt_hi", [P, 2, DC, GT], F32R), msb("qt_lo", [P, 2, DC, GT], F32R)
        kt_hi, kt_lo = msb("kt_hi", [P, 2, DC, GS, SP1], F32R), msb("kt_lo", [P, 2, DC, GS, SP1], F32R)
        vt = msb("vt", [P, DC, GT])
        v2 = msb("v2", [S, 2, GS, H, VW], F32R)
        kbd_hi, kbd_lo = msb("kbd_hi", [P, DC, HC, SP1], F32R), msb("kbd_lo", [P, DC, HC, SP1], F32R)
        rowmax = msb("rowmax", [S, 2, HC])
        probs = msb("probs", [S, 2, HC * SP1])
        pt_hi, pt_lo = msb("pt_hi", [S, 2, HC, SP1], F32R), msb("pt_lo", [S, 2, HC, SP1], F32R)
        otmp = msb("otmp", [S, HC, HD])
        osum = msb("osum", [S, HC, HD])
        rden = msb("rden", [S, 2, HC])
        o_nat = msb("o_nat", [S, D])
        mid.close()

        block = ctx.enter_context(nc.Block())

        PAIRS = TILES // 2
        PATCH_PAIRS = PATCH_TILES // 2
        QUADS = PATCH_PAIRS
        LAST = TILES - 1

        def token_columns(view, pair, j):
            if isinstance(pair, int):
                tile = 2 * pair + j
                if tile == PATCH_TILES:
                    return view[:, :, 0:NPATCH + 2:NPATCH + 1, :]
                if tile == LAST:
                    return view[:, :, S - 1:S, :]
                first = 2 * tile + (1 if tile < PATCH_TILES else 0)
                return view[:, :, first:first + 2, :]
            raise ValueError(pair)

        def looped_columns(view, pair, j, patch):
            return view[:, :, bass.ds(pair * 4 + 2 * j + (1 if patch else 0), 2), :]

        def pairs(engine, step):
            step(0, lambda v, j: token_columns(v, 1, j))
            with engine.Fori(1, PATCH_PAIRS - 1) as n:
                step(n, lambda v, j: looped_columns(v, n + 1, j, True))
            step(PATCH_PAIRS - 1, lambda v, j: token_columns(v, PATCH_PAIRS, j))
            with engine.Fori(PATCH_PAIRS, PAIRS - 1) as n:
                step(n, lambda v, j: looped_columns(v, n + 1, j, False))
            step(PAIRS - 1, lambda v, j: token_columns(v, PAIRS, j))

        E_BANK, T_BANK, CLASS_BANK = 0, 3, 7
        ROUNDS = PATCH_TILES // XSLOT
        PB = XSLOT // 2

        def embed_bank(slot):
            return psum[:, E_BANK + slot, :].rearrange("p (j d) -> p j d", j=2)

        def turned_bank(text):
            return psum[:, T_BANK + text, :].rearrange("p (c j r) -> p c j r", c=DC, j=2)

        PT_BANK, O_BANK, M_BANK = 4, 6, 7
        M = psum[:, M_BANK, :]

        def projection_bank(g, step):
            return psum[:, step, :] if isinstance(g, int) and g == 0 else M

        def last_bank_free(pe, g, kind, step, last_group=False):
            order = []
            for at in range(STEPS):
                if at % 2 and not (isinstance(g, int) and g == 0 and at == 1):
                    order.append(("out", at))
                if at == 2:
                    order.append(("expert", at))
                if not last_group:
                    order.append(("proj", at))
            at = order.index((kind, step)) if kind else len(order)
            if at:
                kind, step = order[at - 1]
                nxt = g + 1
            else:
                kind, step, nxt = "proj", STEPS - 1, g
            if kind == "out":
                pe.wait_ge(ot_done, g * GS + step // 2)
            elif kind == "expert":
                pe.wait_ge(me_done, g + 1)
            else:
                projected(pe, nxt, step)

        def projected(pe, g, step):
            semaphore = (q_ready, k_ready, vt_ready, v_ready)[step // 2]
            pe.wait_ge(semaphore, g * 2 + (step % 2 + 1))

        def group_pairs(engine, group):
            with engine.Fori(0, (GROUPS - 2) // 2) as r:
                group(r * 2 + 1, 1, r)
                group(r * 2 + 2, 0, r + 1)

        def group_columns(g):
            if isinstance(g, int):
                return feat_flat[:, :, g * GT:(g + 1) * GT]
            return feat_flat[:, :, bass.ds(g * GT, GT)]

        def sample_columns(sample):
            if isinstance(sample, int):
                return feat_flat[:, :, sample * S:(sample + 1) * S]
            return feat_flat[:, :, bass.ds(sample * S, S)]

        def me_slice(t, e, half):
            if isinstance(e, int):
                return t[:, half, e, :]
            return t[:, half, bass.ds(e, 1), :].rearrange("p o d -> p (o d)")

        def pt_banks():
            return psum[0:S, PT_BANK:PT_BANK + 2, 0:QUAD * SP1].rearrange("p b (h q) -> p b h q", q=SP1)[:, :, :, 0:S]

        def o_bank():
            return psum[0:S, O_BANK, 0:HC * VW].rearrange("p (h v) -> p h v", v=VW)

        def hid_tile(n, j, rows=P):
            if isinstance(n, int):
                return hid[0:rows, 2 * n + j, :]
            return hid[0:rows, bass.ds(n * 2 + j, 1), :].rearrange("p o d -> p (o d)")

        @block.sync
        def _(sp):
            def load_x(n):
                sp.dma_start(xs[:, 2 * n:2 * n + 2], x_t[2 * n:2 * n + 2].rearrange("i p c t -> p i c t")
                             ).then_inc(x_in[n], 16)

            sp.dma_start(wp[:], w_patch).then_inc(w_in_sem, 16)
            sp.dma_start(posb_s[:], posb).then_inc(w_in_sem, 16)
            sp.dma_start(sel_s[:], sel).then_inc(w_in_sem, 16)
            load_x(0)
            sp.dma_start(hid[:, PATCH_TILES:PATCH_TILES + 2, :], base[0:2 * P].rearrange("(i p) d -> p i d", p=P)
                         ).then_inc(first_base_in, 16)
            sp.dma_start(ident[:], ident_d).then_inc(c_in, 16)
            sp.dma_start(head_mask[:], head_mask_d).then_inc(c_in, 16)
            sp.dma_start(iota[:], iota_d).then_inc(c_in, 16)
            sp.dma_start(bias_l[:], bias_l_d).then_inc(c_in, 16)
            sp.dma_start(bias_r[:], bias_r_d).then_inc(c_in, 16)
            load_x(1)
            sp.dma_start(hid[:, PATCH_TILES + 2:LAST, :], base[2 * P:(LAST - PATCH_TILES) * P].rearrange(
                "(i p) d -> p i d", p=P)).then_inc(base_in, 16)
            sp.dma_start(hid[0:B, LAST, :], base[(LAST - PATCH_TILES) * P:]).then_inc(base_in, 16)
            load_x(2)
            sp.dma_start(raw_qkv[:], w_qkv).then_inc(wq_in, 16)
            sp.dma_start(raw_o[:], w_o).then_inc(wq_in, 16)
            sp.dma_start(raw_g[:], w_g).then_inc(wq_in, 16)
            sp.dma_start(win_s[:], w_in[0]).then_inc(exp_in, 16)
            sp.dma_start(wout_s[:], w_out[0]).then_inc(exp_in, 16)
            with sp.Fori(1, PATCH_TILES // XSLOT) as r:
                for n in range(XSLOT // 2):
                    sp.wait_ge(emb_ready, r * PB + (n + 1 - PB))
                    sp.dma_start(xs[:, 2 * n:2 * n + 2],
                                 x_t[bass.ds(r * XSLOT + 2 * n, 2)].rearrange("i p c t -> p i c t")
                                 ).then_inc(x_in[n], 16)
            with sp.Fori(1, E) as e:
                sp.wait_ge(me_ready, e * 2)
                sp.dma_start(win_s[:], w_in[bass.ds(e, 1)].rearrange("e p j d -> p (e j) d")).then_inc(exp_in, 16)
                sp.dma_start(wout_s[:], w_out[bass.ds(e, 1)].rearrange("e p j d -> p (e j) d")).then_inc(exp_in, 16)

            def store(n, token_of):
                for j in range(2):
                    sp.wait_ge(sum_ready, n * 2 + (j + 1))
                    for u in range(2):
                        src = hid[B * u:B * u + B, bass.ds(n * 2 + j, 1), :].rearrange("b o d -> b (o d)")
                        sp.dma_start(out[:, token_of(j, u), :].rearrange("b o d -> b (o d)"), src
                                     ).then_inc(out_done, 16)

            with sp.Fori(0, PATCH_PAIRS) as n:
                store(n, lambda j, u: bass.ds(n * 4 + (2 * j + u + 1), 1))
            store(PATCH_PAIRS, lambda j, u: [slice(0, 1), slice(NPATCH + 1, NPATCH + 2)][u] if j == 0
                  else slice(2 * PATCH_TILES + 2 + u, 2 * PATCH_TILES + 3 + u))
            with sp.Fori(PATCH_PAIRS + 1, PAIRS) as n:
                store(n, lambda j, u: bass.ds(n * 4 + (2 * j + u), 1))
            sp.wait_ge(sum_ready, TILES)
            sp.dma_start(out[:, S - 1, :], hid[0:B, LAST, :]).then_inc(out_done, 16)
            sp.wait_ge(out_done, 16 * S)

        @block.tensor
        def _(pe):
            mm = nc.tensor.matmul

            def mm3(dst, l_hi, l_lo, r_hi, r_lo, start, stop):
                mm(dst, l_hi, r_hi, start=start, stop=False)
                mm(dst, l_lo, r_hi, start=False, stop=False)
                return mm(dst, l_hi, r_lo, start=False, stop=stop)

            def position(tile):
                if isinstance(tile, int):
                    return posb_s[:, tile, :]
                return posb_s[:, bass.ds(tile, 1), :].rearrange("p o d -> p (o d)")

            def embed(n, slot):
                after(pe, emb_read, n - (PB - 1))
                for j in range(2):
                    dst = embed_bank(slot)[:, j, :]
                    mm(dst, sel_s[:, 0, :], position(n * 2 + j), start=True, stop=False)
                    for c in range(KP):
                        last = mm(dst, xs[:, 2 * slot + j, c, :], wp[:, c, :], start=False, stop=c == KP - 1)
                last.then_inc(emb_ready, 1)

            def turn(n, others=(P, P)):
                pe.wait_ge(normed_ready, n + 1)
                after(pe, feat_ready, n)
                for j, r in enumerate((P, P) + others):
                    for c in range(DC):
                        last = nc.tensor.transpose(turned_bank(j // 2)[:, c, j % 2, 0:r],
                                                   normed[0:r, j, c * P:(c + 1) * P], ident[0:r, 0:r])
                last.then_inc(normed_used, 1)

            pe.wait_ge(w_in_sem, 48)
            mm(psum[:, CLASS_BANK, 0:D], sel_s[:, 1, :], position(PATCH_TILES), start=True, stop=True
               ).then_inc(class_ready, 1)
            for n in range(PB):
                pe.wait_ge(x_in[n], 16)
                embed(n, n)
                if n == 0:
                    pe.wait_ge(c_in, 80)
                else:
                    turn(n - 1)
            with pe.Fori(1, ROUNDS) as r:
                for n in range(PB):
                    pe.wait_ge(x_in[n], r * 16 + 16)
                    embed(r * PB + n, n)
                    turn(r * PB + (n - 1))
            turn(QUADS - 1, (B,))

            def project(g, m):
                if m == 0:
                    pe.wait_ge(xs_lo, g + 1)
                for c in range(DC):
                    w = slice(m * P, (m + 1) * P)
                    last = mm3(projection_bank(g, m)[:, 0:GT], wqkv_hi[:, c, w], wqkv_lo[:, c, w], xg_hi[:, c, :], xg_lo[:, c, :],
                               c == 0, c == DC - 1)
                last.then_inc(proj_ready, 1)

            def turn_v(g, half):
                bank = projection_bank(g, 3 * DC + half)
                pe.wait_ge(vt_ready, g * 2 + 2)
                for s in range(2):
                    for c in range(DC):
                        t0 = (2 * half + s) * S
                        last = nc.tensor.transpose(bank[0:S, s * D + c * P:s * D + (c + 1) * P],
                                                   vt[:, c, t0:t0 + S], ident[:])
                last.then_inc(proj_ready, 1)

            def misc(g, step):
                if step < 3 * DC:
                    project(g, step)
                else:
                    turn_v(g, step - 3 * DC)

            def scores(par, step, s):
                c, sample = step % DC, step // DC
                pe.wait_ge(kbd_ready, s + 1)
                after(pe, probs_ready, s - 1)
                for quad in range(HC // QUAD):
                    dst = psum[0:S, 2 * c + quad, 0:QUAD * SP1]
                    lhs = slice(sample * S, (sample + 1) * S)
                    hs = slice(quad * QUAD, (quad + 1) * QUAD)
                    b0 = (c * HC + quad * QUAD) * SP1
                    mm(dst, bias_l[:], bias_r[:, b0:b0 + QUAD * SP1], start=True, stop=False)
                    last = mm3(dst, qt_hi[:, par, c, lhs], qt_lo[:, par, c, lhs],
                               kbd_hi[:, c, hs, :].rearrange("p h k -> p (h k)"),
                               kbd_lo[:, c, hs, :].rearrange("p h k -> p (h k)"), False, True)
                last.then_inc(s_ready, 1)

            def turn_probs(step, s):
                c = step % DC
                pe.wait_ge(probs_ready, s + 1)
                after(pe, pt_lo_done, s)
                for h in range(HC):
                    q0 = (h % QUAD) * SP1
                    last = nc.tensor.transpose(psum[0:S, PT_BANK + h // QUAD, q0:q0 + S],
                                               probs[:, c, h * SP1:h * SP1 + S], ident[0:S, 0:S])
                last.then_inc(pt_ready, 1)

            def weigh(par, step, s):
                c, sample = step % DC, step // DC
                pe.wait_ge(pt_lo_done, s + 1)
                after(pe, o_read, s)
                for h in range(HC):
                    dst = psum[0:S, O_BANK, h * VW:(h + 1) * VW]
                    rhs = v2[:, par, sample, c * HC + h, :]
                    mm(dst, pt_hi[:, c, h, 0:S], rhs, start=True, stop=False)
                    last = mm(dst, pt_lo[:, c, h, 0:S], rhs, start=False, stop=True)
                last.then_inc(pv_ready, 1)

            def turn_out(sample):
                pe.wait_ge(on_ready, sample * 2 + 2)
                for c in range(DC):
                    last = nc.tensor.transpose(M[:, c * S:(c + 1) * S], o_nat[:, c * P:(c + 1) * P], ident[0:S, 0:S])
                last.then_inc(ot_ready, 1)

            def expert(e, mc):
                pe.wait_ge(exp_in, e * 32 + 32)
                for j in range(JC):
                    last = mm(M[:, 0:D], win_s[:, j, mc * P:(mc + 1) * P], wout_s[:, j, :],
                              start=j == 0, stop=j == JC - 1)
                last.then_inc(me_ready, 1)

            def group(g, par, e, last_group=False):
                for step in range(STEPS):
                    s = g * STEPS + step
                    nxt = (step + 1) % STEPS
                    if not (last_group and step == STEPS - 1):
                        if nxt == 0:
                            pe.wait_ge(q_ready, g * DC + 2 * DC)
                        scores(par if nxt else 1 - par, nxt, s + 1)
                    turn_probs(step, s)
                    if step % 2 and not (isinstance(g, int) and g == 0 and step == 1):
                        last_bank_free(pe, g, "out", step, last_group)
                        turn_out(g * GS + (step // 2 - 1))
                    if step == 2:
                        last_bank_free(pe, g, "expert", step, last_group)
                        expert(e, par)
                    if not (isinstance(g, int) and g == 0 and step == 0):
                        weigh(par if step else 1 - par, (step - 1) % STEPS, s - 1)
                    if not last_group:
                        last_bank_free(pe, g, "proj", step)
                        misc(g + 1, step)
                    if step == 0:
                        pe.wait_ge(v_ready, g * 2 + 2)

            pe.wait_ge(feat_ready, QUADS)
            pe.wait_ge(w_lo_ready, 3)
            pe.wait_ge(pads_ready, 3)
            for step in range(STEPS):
                misc(0, step)
            pe.wait_ge(q_ready, DC)
            scores(0, 0, 0)
            group(0, 0, 0)
            group_pairs(pe, group)
            group(GROUPS - 1, 1, E - 1, last_group=True)
            weigh(1, STEPS - 1, GROUPS * STEPS - 1)
            last_bank_free(pe, GROUPS - 1, None, None, True)
            turn_out(B - 1)

            pe.wait_ge(ot_done, B)
            pe.wait_ge(me_done, GROUPS)

            def out_projection(i, j, rows=P):
                pe.wait_ge(of_lo, i + 1)
                after(pe, mid_ready, i)
                for c in range(DC):
                    last = mm3(psum[0:rows, 4, 0:D], of_h[:, j, c, 0:rows], of_l[:, j, c, 0:rows],
                               wo_hi[:, c, :], wo_lo[:, c, :], c == 0, c == DC - 1)
                last.then_inc(wo_ready, 1)

            def turn_mid(i, j, rows=P):
                pe.wait_ge(n2_ready, i + 1)
                after(pe, x2_lo, i)
                for c in range(DC):
                    last = nc.tensor.transpose(psum[:, 5, c * P:c * P + rows], normed[0:rows, j, c * P:(c + 1) * P],
                                               ident[0:rows, 0:rows])
                last.then_inc(x2t_ready, 1)

            def gate(i, j, rows=P):
                pe.wait_ge(x2_lo, i + 1)
                after(pe, g_read, i)
                for c in range(DC):
                    last = mm3(psum[0:rows, 6, 0:E], x2_h[:, j, c, 0:rows], x2_l[:, j, c, 0:rows],
                               wg_hi[:, c, :], wg_lo[:, c, :], c == 0, c == DC - 1)
                last.then_inc(g_ready, 1)

            def experts(i, j, e2, rows=P):
                if 2 * e2 < DVE_E:
                    after(pe, moe_read, i * DVE_E + (2 * e2 + 2 - DVE_E))
                else:
                    after(pe, scaled_ready, i * (E - DVE_E) + (2 * e2 + 2 - E))
                for c in range(DC):
                    last = mm3(psum[0:rows, e2, :], x2_h[:, j, c, 0:rows], x2_l[:, j, c, 0:rows],
                               me_hi[:, c, 2 * e2:2 * e2 + 2, :].rearrange("p e d -> p (e d)"),
                               me_lo[:, c, 2 * e2:2 * e2 + 2, :].rearrange("p e d -> p (e d)"),
                               c == 0, c == DC - 1)
                last.then_inc(moe_ready, 1)

            def tile3(i, j, rows=P, rows1=P, rows2=P):
                experts(i, j, 0, rows)
                experts(i, j, 1, rows)
                if rows1:
                    turn_mid(i + 1, 1 - j, rows1)
                experts(i, j, 2, rows)
                if rows1:
                    gate(i + 1, 1 - j, rows1)
                if rows2:
                    out_projection(i + 2, j, rows2)
                experts(i, j, 3, rows)

            def pair3(n, columns):
                last_pair = isinstance(n, int) and n == PAIRS - 1
                tile3(n * 2, 0, rows2=B if last_pair else P)
                tile3(n * 2 + 1, 1, rows1=B if last_pair else P, rows2=0 if last_pair else P)

            out_projection(0, 0)
            out_projection(1, 1)
            turn_mid(0, 0)
            gate(0, 0)
            pairs(pe, pair3)
            tile3(LAST, 0, rows=B, rows1=0, rows2=0)

        @block.scalar
        def _(act):
            nc.scalar.preload_act_table_set("natural_log_exp_and_others")

            def copy(dst, src, scale=1.0):
                return nc.scalar.activation(dst, src, ACT.Copy, scale=scale)

            def guess(n, j=0, width=2, rows=P):
                act.wait_ge(var_ready, n + 1)
                v, lg, g = (root[0:rows, k, j:j + width] for k in range(3))
                nc.scalar.activation(lg, v, ACT.Ln).then_inc(log_ready, 1)
                act.wait_ge(log_ready, n + 1)
                nc.scalar.activation(g, lg, ACT.Exp, scale=-0.5).then_inc(guess_ready, 1)

            def embedded(n, slot):
                act.wait_ge(emb_ready, n + 1)
                copy(hid[:, bass.ds(n * 2, 2), :], embed_bank(slot)).then_inc(emb_read, 1)

            def turned(n, patches, others):
                act.wait_ge(normed_used, n + 1)
                copy(patches, turned_bank(0).rearrange("p c j (t b) -> p c (j t) b", b=B))
                for dst, src in others:
                    last = copy(dst, src)
                last.then_inc(feat_ready, 1)

            def turned_whole(n):
                turned(n, feat_tb[:, :, bass.ds(n * 4 + 1, 4), :],
                       [(feat_tb[:, :, bass.ds(n * 4 + 4 * PATCH_PAIRS, 4), :],
                         turned_bank(1).rearrange("p c j (t b) -> p c (j t) b", b=B))])

            for n in range(PB):
                embedded(n, n)
                guess(n, 0, 4)
                if n == 1:
                    turned(0, feat_tb[:, :, 1:5, :],
                           [(token_columns(feat_tb, PATCH_PAIRS, j),
                             turned_bank(1)[:, :, j, :].rearrange("p c (t b) -> p c t b", b=B)) for j in range(2)])
                elif n:
                    turned_whole(n - 1)
            act.wait_ge(wq_in, 48)
            for dst, src in ((wqkv_hi, raw_qkv), (wo_hi, raw_o), (wg_hi, raw_g)):
                copy(dst[:], src[:]).then_inc(w_hi_ready, 1)
            with act.Fori(1, ROUNDS) as r:
                for n in range(PB):
                    embedded(r * PB + n, n)
                    turned_whole(r * PB + (n - 1))
                    guess(r * PB + n, 0, 4)
            turned(QUADS - 1, feat_tb[:, :, 4 * QUADS - 3:4 * QUADS + 1, :],
                   [(feat_tb[:, :, S - 1, :], turned_bank(1)[:, :, 0, 0:B])])

            def misc(g, par, step):
                bank = projection_bank(g, step)
                if step < 2 * DC:
                    act.wait_ge(proj_ready, g * STEPS + (step + 1))
                    if step < DC:
                        copy(qt_hi[:, par, step, :], bank[:, 0:GT], HD ** -0.5).then_inc(proj_hi, 1)
                    else:
                        copy(kt_hi[:, par, step - DC, :, 0:S], bank[:, 0:GT].rearrange("p (s t) -> p s t", s=GS)).then_inc(proj_hi, 1)
                elif step < 3 * DC:
                    act.wait_ge(proj_ready, g * STEPS + (step + 1))
                    copy(vt[:, step - 2 * DC, :], bank[:, 0:GT]).then_inc(vt_ready, 1)
                else:
                    act.wait_ge(proj_ready, g * STEPS + (step + 1))
                    half = step - 3 * DC
                    copy(v2[:, par, 2 * half:2 * half + 2, :, 0:HD],
                         bank[0:S, :].rearrange("p (s h d) -> p s h d", s=2, h=H)).then_inc(proj_hi, 1)

            def exponentials(step, s):
                c = step % DC
                act.wait_ge(max_done, s + 1)
                after(act, pt_ready, s - 1)
                for h in range(QUAD):
                    nc.scalar.activation(probs[:, c, (QUAD + h) * SP1:(QUAD + h) * SP1 + S],
                                         psum[0:S, 2 * c + 1, h * SP1:h * SP1 + S], ACT.Exp,
                                         bias=rowmax[:, c, QUAD + h:QUAD + h + 1])
                act.wait_ge(shifted_ready, s + 1)
                quad = probs[:, c, 0:QUAD * SP1]
                nc.scalar.activation(quad, quad, ACT.Exp).then_inc(probs_ready, 1)

            def probs_hi(step, s):
                c = step % DC
                act.wait_ge(pt_ready, s + 1)
                after(act, pv_ready, s - 1)
                copy(pt_hi[:, c, :, 0:S].rearrange("p (b h) q -> p b h q", b=2), pt_banks()).then_inc(pt_hi_done, 1)

            def out_low(s):
                act.wait_ge(pv_ready, s + 1)
                after(act, o_read, s)
                copy(otmp[:], o_bank()[:, :, HD:2 * HD]).then_inc(otmp_ready, 1)

            def out_turned(sample):
                act.wait_ge(ot_ready, sample + 1)
                copy(sample_columns(sample), M[:, 0:DC * S].rearrange("p (c t) -> p c t", c=DC)
                     ).then_inc(ot_done, 1)

            def expert(g, e, par):
                act.wait_ge(me_ready, g + 1)
                copy(me_slice(me_hi, e, par), M[:, 0:D]).then_inc(me_hi_done, 1)

            def group(g, par, e, last_group=False):
                for step in range(STEPS):
                    s = g * STEPS + step
                    probs_hi(step, s)
                    if step % 2 and not (isinstance(g, int) and g == 0 and step == 1):
                        out_turned(g * GS + (step // 2 - 1))
                    if not (last_group and step == STEPS - 1):
                        exponentials((step + 1) % STEPS, s + 1)
                    if step == 2:
                        expert(g, e, par)
                    if not (isinstance(g, int) and g == 0 and step == 0):
                        out_low(s - 1)
                    if not last_group:
                        misc(g + 1, 1 - par, step)

            act.wait_ge(feat_ready, QUADS)
            act.wait_ge(w_lo_ready, 3)
            act.wait_ge(pads_ready, 3)
            copy(xg_hi[:], group_columns(0)).then_inc(xs_hi, 1)
            for step in range(STEPS):
                if step == 3 * DC:
                    act.wait_ge(proj_ready, 3 * DC)
                    copy(xg_hi[:], group_columns(1)).then_inc(xs_hi, 1)
                misc(0, 0, step)
            exponentials(0, 0)
            group(0, 0, 0)
            group_pairs(act, group)
            group(GROUPS - 1, 1, E - 1, last_group=True)
            out_low(GROUPS * STEPS - 1)
            out_turned(B - 1)

            def spread(i, j, src):
                after(act, wo_ready, i - 1)
                copy(of_h[:, j].rearrange("p c (t b) -> p c t b", b=B)[:, :, 0:src.shape[2], :], src
                     ).then_inc(of_hi, 1)

            def mid_hi(i, j, rows=P):
                act.wait_ge(x2t_ready, i + 1)
                after(act, moe_ready, i * 4 - 4)
                copy(x2_h[:, j, :, 0:rows], psum[:, 5, 0:D].rearrange("p (c r) -> p c r", c=DC)[:, :, 0:rows]
                     ).then_inc(x2_hi, 1)

            def gate_exp(i, rows=P):
                act.wait_ge(gd_ready, i + 1)
                nc.scalar.activation(gtmp[0:rows, 2, 1:2], gtmp[0:rows, 2, 0:1], ACT.Exp).then_inc(ge_ready, 1)

            def scale(i, j, e2, rows=P):
                act.wait_ge(moe_ready, i * 4 + (e2 + 1))
                act.wait_ge(gates_ready, i + 1)
                for e in (2 * e2, 2 * e2 + 1):
                    after(act, part_ready, i * 3 - (0 if e == E - 1 else 1 if e == E - 2 else 2))
                    nc.scalar.activation(scaled[0:rows, e - DVE_E, :],
                                         psum[0:rows, e2, (e % 2) * D:(e % 2 + 1) * D], ACT.Copy,
                                         scale=gtmp[0:rows, 6 + j, e:e + 1]).then_inc(scaled_ready, 1)

            def tile3(i, j, rows=P, rows1=P, rows2=P, ahead=None):
                if ahead is not None:
                    spread(i + 2, j, ahead)
                if rows1:
                    mid_hi(i + 1, 1 - j, rows1)
                scale(i, j, 2, rows)
                if rows1:
                    gate_exp(i + 1, rows1)
                if rows2:
                    guess(i + (QUADS + 2), j, 1, rows2)
                scale(i, j, 3, rows)

            def pair3(n, columns):
                last_pair = isinstance(n, int) and n == PAIRS - 1
                tile3(n * 2, 0, rows2=B if last_pair else P, ahead=columns(feat_tb, 0))
                tile3(n * 2 + 1, 1, rows1=B if last_pair else P, rows2=0 if last_pair else P,
                      ahead=None if last_pair else columns(feat_tb, 1))

            act.wait_ge(me_done, GROUPS)
            act.wait_ge(ot_done, B)
            for j in range(2):
                spread(j, j, token_columns(feat_tb, 0, j))
            guess(QUADS, 0, 1)
            mid_hi(0, 0)
            gate_exp(0)
            guess(QUADS + 1, 1, 1)
            pairs(act, pair3)
            tile3(LAST, 0, rows=B, rows1=0, rows2=0)

        @block.gpsimd
        def _(pool):
            pool.wait_ge(w_hi_ready, 3)
            for lo, raw, hi in ((wqkv_lo, raw_qkv, wqkv_hi), (wo_lo, raw_o, wo_hi), (wg_lo, raw_g, wg_hi)):
                nc.gpsimd.tensor_tensor(out=lo[:], in0=raw[:], in1=hi[:], op=ALU.subtract).then_inc(w_lo_ready, 1)
            pool.wait_ge(feat_ready, QUADS)
            pool.wait_ge(w_lo_ready, 3)
            nc.gpsimd.memset(kt_hi[:, :, :, :, S:SP1].bitcast(F32), 0.0).then_inc(pads_ready, 1)
            nc.gpsimd.memset(kt_lo[:, :, :, :, S:SP1].bitcast(F32), 0.0).then_inc(pads_ready, 1)
            nc.gpsimd.memset(v2[:, :, :, :, 2 * HD:VW].bitcast(F32), 1.0).then_inc(pads_ready, 1)
            pool.wait_ge(pads_ready, 3)
            pool.wait_ge(c_in, 80)

            def spread_keys(g, par, step, s):
                c, sample = step % DC, step // DC
                if sample == 0:
                    pool.wait_ge(k_ready, g * DC + DC)
                after(pool, s_ready, s - 1)
                mask = head_mask[:].rearrange("p (h o) -> p h o", o=1).to_broadcast([P, HC, SP1])
                for dst, src in ((kbd_hi, kt_hi), (kbd_lo, kt_lo)):
                    k = src[:, par, c, sample, :].rearrange("p (o k) -> p o k", o=1).to_broadcast([P, HC, SP1])
                    last = nc.gpsimd.tensor_tensor(out=dst[:, c], in0=k, in1=mask, op=ALU.mult)
                last.then_inc(kbd_ready, 1)

            def split_hi(g):
                after(pool, proj_ready, g * STEPS + (3 * DC - STEPS))
                nc.gpsimd.tensor_copy(xg_hi[:], group_columns(g)).then_inc(xs_hi, 1)

            def split_lo(g):
                nc.gpsimd.tensor_tensor(out=xg_lo[:], in0=group_columns(g), in1=xg_hi[:], op=ALU.subtract
                                        ).then_inc(xs_lo, 1)

            def group(g, par, e, last_group=False):
                for step in range(STEPS):
                    later = (step + 2) % STEPS
                    s = g * STEPS + step + 2
                    splits = step == 0 and not last_group and not isinstance(g, int)
                    if splits:
                        split_hi(g + 1)
                        pool.wait_ge(xs_hi, g + 2)
                    if step + 2 < STEPS:
                        spread_keys(g, par, later, s)
                    elif not last_group:
                        spread_keys(g + 1, 1 - par, later, s)
                    if splits:
                        split_lo(g + 1)

            spread_keys(0, 0, 0, 0)
            spread_keys(0, 0, 1, 1)
            group(0, 0, 0)
            group_pairs(pool, group)
            group(GROUPS - 1, 1, E - 1, last_group=True)

            def spread(i, j, src):
                pool.wait_ge(of_hi, i + 1)
                r = src.shape[2]
                nc.gpsimd.tensor_tensor(out=of_l[:, j].rearrange("p c (t b) -> p c t b", b=B)[:, :, 0:r, :], in0=src,
                                        in1=of_h[:, j].rearrange("p c (t b) -> p c t b", b=B)[:, :, 0:r, :],
                                        op=ALU.subtract).then_inc(of_lo, 1)

            def total(i, tile, rows=P):
                p, q = part[0:rows, 0, :], part[0:rows, 1, :]
                pool.wait_ge(scaled_ready, i * (E - DVE_E) + 2)
                after(pool, sum_ready, i)
                nc.gpsimd.tensor_tensor(out=p, in0=scaled[0:rows, 0, :], in1=scaled[0:rows, 1, :], op=ALU.add
                                        ).then_inc(part_ready, 1)
                pool.wait_ge(scaled_ready, i * (E - DVE_E) + 4)
                nc.gpsimd.tensor_tensor(out=q, in0=scaled[0:rows, 2, :], in1=scaled[0:rows, 3, :], op=ALU.add
                                        ).then_inc(part_ready, 1)
                pool.wait_ge(part_ready, i * 3 + 2)
                nc.gpsimd.tensor_tensor(out=p, in0=p, in1=q, op=ALU.add).then_inc(part_ready, 1)
                pool.wait_ge(part_ready, i * 3 + 3)
                pool.wait_ge(moe_read, i * DVE_E + DVE_E)
                nc.gpsimd.tensor_tensor(out=tile, in0=p, in1=tile, op=ALU.add).then_inc(sum_ready, 1)

            def pair3(n, columns):
                last_pair = isinstance(n, int) and n == PAIRS - 1
                for j in range(2):
                    if not (last_pair and j):
                        spread(n * 2 + (2 + j), j, columns(feat_tb, j))
                    total(n * 2 + j, hid_tile(n, j))

            for j in range(2):
                spread(j, j, token_columns(feat_tb, 0, j))
            pairs(pool, pair3)
            total(LAST, hid_tile(PAIRS, 0, B), B)

        @block.vector
        def _(dve):
            tt = nc.vector.tensor_tensor

            def moments(stats_ready, count, total, tiles):
                w = 1 if len(tiles) == 1 else 4
                for j, r, source in tiles:
                    last = nc.vector.bn_stats(stats[0:r, j, :], source)
                last.then_inc(stats_ready, 1)
                dve.wait_ge(c_in, 80)
                dve.wait_ge(stats_ready, count)
                for j, r, source in tiles:
                    last = nc.vector.bn_aggr(mv[0:r, j, :], stats[0:r, j, :])
                last.then_inc(aggr_ready, 1)
                dve.wait_ge(aggr_ready, total + 1)
                j0, r = tiles[0][0], tiles[0][1]
                nc.vector.tensor_scalar_add(root[0:r, 0, j0:j0 + w], mv[0:r, j0:j0 + w, 1], EPS
                                            ).then_inc(var_ready, 1)

            def normalised(chain, count, tiles, used, done):
                j0, r, w = tiles[0][0], tiles[0][1], 1 if len(tiles) == 1 else 4
                v, g = root[0:r, 0, j0:j0 + w], root[0:r, 2, j0:j0 + w]
                rs = rstd[0:r, j0:j0 + w]
                dve.wait_ge(guess_ready, count + 1)
                tt(out=rs, in0=g, in1=g, op=ALU.mult).then_inc(dve_chain, 1)
                dve.wait_ge(dve_chain, chain + 1)
                nc.vector.scalar_tensor_tensor(out=rs, in0=rs, scalar=-0.5, in1=v, op0=ALU.mult, op1=ALU.mult
                                               ).then_inc(dve_chain, 1)
                dve.wait_ge(dve_chain, chain + 2)
                nc.vector.scalar_tensor_tensor(out=rs, in0=rs, scalar=1.5, in1=g, op0=ALU.add, op1=ALU.mult
                                               ).then_inc(dve_chain, 1)
                dve.wait_ge(dve_chain, chain + 3)
                used()
                for j, r, source in tiles:
                    last = nc.vector.tensor_scalar(normed[0:r, j, :], source, mv[0:r, j, 0:1], rstd[0:r, j:j + 1],
                                                   ALU.subtract, ALU.mult)
                last.then_inc(done, 1)

            def norm1(n, others=(P, P)):
                tiles = [(j, P, hid_tile(n, j)) for j in range(2)]
                tiles += [(2 + j, r, hid_tile(n + PATCH_PAIRS, j, r)) for j, r in enumerate(others)]
                dve.wait_ge(emb_read, n + 1)
                moments(stats1, n + 1, n, tiles)
                normalised(n * 3, n, tiles, lambda: after(dve, normed_used, n), normed_ready)

            dve.wait_ge(class_ready, 1)
            dve.wait_ge(first_base_in, 16)
            dve.wait_ge(c_in, 80)
            tt(out=hid_tile(PATCH_PAIRS, 0, B), in0=psum[0:B, CLASS_BANK, 0:D], in1=hid_tile(PATCH_PAIRS, 0, B),
               op=ALU.add).then_inc(class_ready, 1)
            dve.wait_ge(class_ready, 2)
            norm1(0)
            dve.wait_ge(base_in, 32)
            with dve.Fori(1, QUADS - 1) as n:
                norm1(n)
            norm1(QUADS - 1, (B,))

            def misc(g, par, step):
                bank = projection_bank(g, step)
                if step < DC:
                    dve.wait_ge(proj_hi, g * 6 + (step + 1))
                    nc.vector.scalar_tensor_tensor(out=qt_lo[:, par, step, :], in0=bank[:, 0:GT], scalar=HD ** -0.5,
                                                   in1=qt_hi[:, par, step, :], op0=ALU.mult, op1=ALU.subtract
                                                   ).then_inc(q_ready, 1)
                    return "q"
                if step < 2 * DC:
                    dve.wait_ge(proj_hi, g * 6 + (step + 1))
                    tt(out=kt_lo[:, par, step - DC, :, 0:S], in0=bank[:, 0:GT].rearrange("p (s t) -> p s t", s=GS),
                       in1=kt_hi[:, par, step - DC, :, 0:S], op=ALU.subtract).then_inc(k_ready, 1)
                elif step >= 3 * DC:
                    half = step - 3 * DC
                    dve.wait_ge(proj_hi, g * 6 + (2 * DC + half + 1))
                    tt(out=v2[:, par, 2 * half:2 * half + 2, :, HD:2 * HD],
                       in0=bank[0:S, :].rearrange("p (s h d) -> p s h d", s=2, h=H),
                       in1=v2[:, par, 2 * half:2 * half + 2, :, 0:HD], op=ALU.subtract).then_inc(v_ready, 1)

            def row_maxima(step, s):
                c = step % DC
                dve.wait_ge(s_ready, s + 1)
                sc = psum[0:S, 2 * c:2 * c + 2, 0:QUAD * SP1].rearrange("p b (h k) -> p b h k", k=SP1)
                mx = rowmax[:, c, :].rearrange("p (b h) -> p b h", b=2)
                after(dve, probs_ready, s - 1)
                nc.vector.tensor_reduce(out=mx, in_=sc[:, :, :, 0:S], op=ALU.max, axis=AX_X, negate=True
                                        ).then_inc(max_done, 1)
                dve.wait_ge(max_done, s + 1)
                after(dve, pt_ready, s - 1)
                tt(out=probs[:, c, 0:QUAD * SP1].rearrange("p (h k) -> p h k", k=SP1), in0=sc[:, 0],
                   in1=mx[:, 0].rearrange("p (h o) -> p h o", o=1).to_broadcast([S, QUAD, SP1]), op=ALU.add
                   ).then_inc(shifted_ready, 1)

            def probs_lo(step, s):
                c = step % DC
                dve.wait_ge(pt_hi_done, s + 1)
                tt(out=pt_lo[:, c, :, 0:S].rearrange("p (b h) q -> p b h q", b=2), in0=pt_banks(),
                   in1=pt_hi[:, c, :, 0:S].rearrange("p (b h) q -> p b h q", b=2), op=ALU.subtract
                   ).then_inc(pt_lo_done, 1)

            def normalise(step, s, sample_turned):
                c = step % DC
                dve.wait_ge(otmp_ready, s + 1)
                after(dve, on_ready, s)
                nc.vector.reciprocal(rden[:, c, :], o_bank()[:, :, 2 * HD])
                tt(out=osum[:], in0=o_bank()[:, :, 0:HD], in1=otmp[:], op=ALU.add).then_inc(o_read, 1)
                dve.wait_ge(o_read, s + 1)
                if sample_turned is not None:
                    after(dve, ot_ready, sample_turned)
                tt(out=o_nat[:, c * P:(c + 1) * P].rearrange("p (h d) -> p h d", h=HC), in0=osum[:],
                   in1=rden[:, c, :].rearrange("p (h o) -> p h o", o=1).to_broadcast([S, HC, HD]), op=ALU.mult
                   ).then_inc(on_ready, 1)

            def expert(g, e, par):
                dve.wait_ge(me_hi_done, g + 1)
                tt(out=me_slice(me_lo, e, par), in0=M[:, 0:D], in1=me_slice(me_hi, e, par), op=ALU.subtract
                   ).then_inc(me_done, 1)

            def group(g, par, e, last_group=False):
                for step in range(STEPS):
                    s = g * STEPS + step
                    if not (last_group and step == STEPS - 1):
                        row_maxima((step + 1) % STEPS, s + 1)
                    probs_lo(step, s)
                    if step == 2:
                        expert(g, e, par)
                    if not (isinstance(g, int) and g == 0 and step == 0):
                        normalise((step - 1) % STEPS, s - 1, g * GS + (step - 1) // 2)
                    if not last_group:
                        misc(g + 1, 1 - par, step)

            dve.wait_ge(xs_hi, 1)
            tt(out=xg_lo[:], in0=group_columns(0), in1=xg_hi[:], op=ALU.subtract).then_inc(xs_lo, 1)
            for step in range(STEPS):
                misc(0, 0, step)
            dve.wait_ge(xs_hi, 2)
            tt(out=xg_lo[:], in0=group_columns(1), in1=xg_hi[:], op=ALU.subtract).then_inc(xs_lo, 1)
            row_maxima(0, 0)
            group(0, 0, 0)
            group_pairs(dve, group)
            group(GROUPS - 1, 1, E - 1, last_group=True)
            normalise(STEPS - 1, GROUPS * STEPS - 1, B - 1)

            base_chain = 3 * QUADS

            def middle(i, j, tile, rows=P):
                dve.wait_ge(wo_ready, i + 1)
                tt(out=tile, in0=psum[0:rows, 4, 0:D], in1=tile, op=ALU.add).then_inc(mid_ready, 1)
                dve.wait_ge(c_in, 80)
                dve.wait_ge(mid_ready, i + 1)
                moments(stats3, i + 1, i + QUADS, [(j, rows, tile)])

            def norm2(i, j, tile, rows=P):
                normalised(i * CH + base_chain, i + QUADS, [(j, rows, tile)], lambda: None, n2_ready)

            CH = 9

            def mid_lo(i, j, rows=P):
                dve.wait_ge(x2_hi, i + 1)
                view = psum[:, 5, 0:D].rearrange("p (c r) -> p c r", c=DC)[:, :, 0:rows]
                tt(out=x2_l[:, j, :, 0:rows], in0=view, in1=x2_h[:, j, :, 0:rows], op=ALU.subtract
                   ).then_inc(x2_lo, 1)

            def link(ins, value):
                ins.then_inc(dve_chain, 1)
                dve.wait_ge(dve_chain, value)

            def top_two(i, j, rows=P):
                r = slice(0, rows)
                dve.wait_ge(g_ready, i + 1)
                nc.vector.tensor_copy(gtmp[r, 0, :], psum[r, 6, 0:E]).then_inc(g_read, 1)
                dve.wait_ge(c_in, 80)
                dve.wait_ge(g_read, i + 1)
                link(nc.vector.max(gtmp[r, 1, :], gtmp[r, 0, :]), i * CH + (base_chain + 4))
                tt(out=gtmp[r, 2, 0:1], in0=gtmp[r, 1, 1:2], in1=gtmp[r, 1, 0:1], op=ALU.subtract
                   ).then_inc(gd_ready, 1)
                link(nc.vector.max_index(gidx[r, :], gtmp[r, 1, :], gtmp[r, 0, :]), i * CH + (base_chain + 5))
                nc.vector.tensor_copy(gtmp[r, 3, 0:2], gidx[r, 0:2])

            def gates(i, j, rows=P):
                r = slice(0, rows)
                chain = i * CH + base_chain
                dve.wait_ge(ge_ready, i + 1)
                link(nc.vector.tensor_scalar_add(gtmp[r, 4, 0:1], gtmp[r, 2, 1:2], 1.0), chain + 6)
                link(nc.vector.reciprocal(gtmp[r, 4, 1:2], gtmp[r, 4, 0:1]), chain + 7)
                tt(out=gtmp[r, 4, 2:3], in0=gtmp[r, 2, 1:2], in1=gtmp[r, 4, 1:2], op=ALU.mult)
                link(nc.vector.tensor_scalar(gtmp[r, 5, :], iota[r, :], gtmp[r, 3, 0:1], gtmp[r, 4, 1:2],
                                             ALU.is_equal, ALU.mult), chain + 8)
                link(nc.vector.tensor_scalar(gtmp[r, 0, :], iota[r, :], gtmp[r, 3, 1:2], gtmp[r, 4, 2:3],
                                             ALU.is_equal, ALU.mult), chain + 9)
                after(dve, scaled_ready, (i - 1) * (E - DVE_E))
                tt(out=gtmp[r, 6 + j, :], in0=gtmp[r, 5, :], in1=gtmp[r, 0, :], op=ALU.add).then_inc(gates_ready, 1)

            def combine(i, j, tile, e2, rows=P):
                dve.wait_ge(moe_ready, i * 4 + (e2 + 1))
                dve.wait_ge(gates_ready, i + 1)
                for e in (2 * e2, 2 * e2 + 1):
                    if e:
                        dve.wait_ge(moe_read, i * DVE_E + e)
                    nc.vector.scalar_tensor_tensor(out=tile, in0=psum[0:rows, e2, (e % 2) * D:(e % 2 + 1) * D],
                                                   scalar=gtmp[0:rows, 6 + j, e:e + 1], in1=tile,
                                                   op0=ALU.mult, op1=ALU.add).then_inc(moe_read, 1)

            def tile3(n, j, rows=P, rows1=P, rows2=P):
                i = n * 2 + j
                tile = hid_tile(n, j, rows)
                if rows1:
                    norm2(i + 1, 1 - j, hid_tile(n + j, 1 - j, rows1), rows1)
                combine(i, j, tile, 0, rows)
                if rows1:
                    mid_lo(i + 1, 1 - j, rows1)
                combine(i, j, tile, 1, rows)
                if rows1:
                    top_two(i + 1, 1 - j, rows1)
                if rows2:
                    middle(i + 2, j, hid_tile(n + 1, j, rows2), rows2)
                if rows1:
                    gates(i + 1, 1 - j, rows1)

            def pair3(n, columns):
                last_pair = isinstance(n, int) and n == PAIRS - 1
                tile3(n, 0, rows2=B if last_pair else P)
                tile3(n, 1, rows1=B if last_pair else P, rows2=0 if last_pair else P)

            dve.wait_ge(ot_done, B)
            middle(0, 0, hid_tile(0, 0))
            norm2(0, 0, hid_tile(0, 0))
            mid_lo(0, 0)
            top_two(0, 0)
            middle(1, 1, hid_tile(0, 1))
            gates(0, 0)
            pairs(dve, pair3)
            tile3(PAIRS, 0, rows=B, rows1=0, rows2=0)


def constants():
    import numpy as np
    bf = np.dtype("bfloat16")

    def parts(a):
        hi = a.astype(bf)
        mid = (a - hi.astype(np.float32)).astype(bf)
        lo = (a - hi.astype(np.float32) - mid.astype(np.float32)).astype(bf)
        return hi, mid, lo

    slopes = (np.float32(1.0) / np.power(np.float32(256.0), (np.arange(H, dtype=np.float32) + 1) / np.float32(H))
              ).astype(np.float32)
    left = np.zeros((NBIAS, S), bf)
    right = np.zeros((NBIAS, H, SP1), bf)
    left[:S] = np.eye(S)
    q, k = np.arange(S), np.arange(SP1)
    right[:S] = np.where((k[None, :] > q[:, None]) | (k[None, :] >= S), np.float32(-2.0 ** 100), 0)[:, None, :]
    for n, part in enumerate(parts(slopes)):
        left[S + n] = q
        right[S + n] = -part[:, None]
    for n, part in enumerate(parts(slopes[:, None] * k.astype(np.float32)[None, :])):
        left[S + 3 + n] = 1
        right[S + 3 + n] = part
    sel = np.zeros((3, 2, P), np.float32)
    sel[0, :, :B] = 1
    sel[1, :, B:] = 1
    sel[2, 0, :] = 1
    mask = (np.arange(P)[:, None] // HD == np.arange(HC)[None, :]).astype(np.float32)
    iota = np.broadcast_to(np.arange(E, dtype=np.float32), (P, E)).copy()
    return {"sel": sel, "ident": np.eye(P, dtype=np.float32), "bias_l": left, "bias_r": right.reshape(NBIAS, -1),
            "head_mask": mask, "iota": iota}


def kernel(x, txt, L0_tok_W, L0_tok_b, L0_tok_class_token, L0_tok_pos_emb, L0_attn_W_Q, L0_attn_W_K, L0_attn_W_V,
           L0_attn_W_O, L0_ffn_w_gate, L0_ffn_w_in, L0_ffn_w_out):
    import numpy as np
    import concourse.bacc as bacc
    from concourse import mybir as mb
    from concourse.bass_utils import run_bass_kernel_spmd

    x, txt = np.asarray(x), np.asarray(txt)
    n = IMG // PATCH
    pat = x.reshape(B, CIN, n, PATCH, n, PATCH).transpose(1, 3, 5, 2, 4, 0).reshape(KP, P, PATCH_TILES, 2 * B)
    pat = np.ascontiguousarray(pat.transpose(2, 1, 0, 3))
    cls = np.broadcast_to(np.asarray(L0_tok_class_token).reshape(1, 1, D), (1, B, D))
    base = np.concatenate([cls, txt.transpose(1, 0, 2)], axis=0).reshape(-1, D)
    pos = np.asarray(L0_tok_pos_emb).reshape(NPATCH + 1, D)
    rows = np.zeros((2 * PATCH_TILES + 2, D), pos.dtype)
    rows[:NPATCH], rows[NPATCH] = pos[1:], pos[0]
    bias = np.broadcast_to(np.asarray(L0_tok_b).reshape(1, 1, D), (1, PATCH_TILES + 1, D))
    posb = np.concatenate([rows.reshape(PATCH_TILES + 1, 2, D).transpose(1, 0, 2), bias], axis=0)

    def by_row(w):
        return np.ascontiguousarray(w.reshape(-1, P, w.shape[1]).transpose(1, 0, 2))

    wq, wk, wv = (np.asarray(w) for w in (L0_attn_W_Q, L0_attn_W_K, L0_attn_W_V))
    inputs = {
        "x_t": pat, "base": base, "posb": posb,
        "w_patch": by_row(np.asarray(L0_tok_W)),
        "w_qkv": by_row(np.concatenate([wq.T, wk.T, wv.T], axis=1)),
        "w_o": by_row(np.asarray(L0_attn_W_O).T),
        "w_g": by_row(np.asarray(L0_ffn_w_gate).T),
        "w_in": np.asarray(L0_ffn_w_in).reshape(E, P, JC, D),
        "w_out": np.ascontiguousarray(np.asarray(L0_ffn_w_out).transpose(0, 2, 1)).reshape(E, P, JC, D),
    }
    inputs.update(constants())
    order = ["x_t", "base", "posb", "sel", "w_patch", "w_qkv", "w_o", "w_g", "w_in", "w_out", "ident", "bias_l",
             "bias_r", "head_mask", "iota"]
    nc = bacc.Bacc("TRN2", target_bir_lowering=False, num_devices=1)
    arrays, aps = {}, []
    for name in order:
        a = np.ascontiguousarray(inputs[name])
        arrays[f"in_{name}"] = a
        aps.append(nc.dram_tensor(f"in_{name}", a.shape, mb.dt.from_np(a.dtype), kind="ExternalInput").ap())
    out = nc.dram_tensor("out", (B, S, D), F32, kind="ExternalOutput").ap()
    fusion_block(nc, *aps, out)
    r = run_bass_kernel_spmd(nc, [arrays], core_ids=[0])
    return r.results[0]["out"]
```

```python
from contextlib import ExitStack

import concourse.bass as bass
from concourse import mybir

ALU = mybir.AluOpType
ACT = mybir.ActivationFunctionType
AX_X = mybir.AxisListType.X
F32 = mybir.dt.float32
F32R = mybir.dt.float32r
BF16 = mybir.dt.bfloat16
U32 = mybir.dt.uint32

P = 128
B, CIN, IMG, PATCH = 64, 3, 96, 16
NPATCH = (IMG // PATCH) ** 2
TXT = 32
S = 1 + NPATCH + TXT
D, H, E, HID = 256, 16, 8, 1024
HD = D // H
DC = D // P
KP = CIN * PATCH * PATCH // P
JC = HID // P
EPS = 1e-5

TILES = (S + 1) // 2
PATCH_TILES = NPATCH // 2
XSLOT = 6
SP1 = S + 1

HC = H // DC
QUAD = 4
GS = 4
GT = GS * S
GROUPS = B // GS
STEPS = GS * DC
EXPERT_STEP = 0
VW = 2 * HD + 2
NBIAS = S + 6
DVE_E = 2
ACT_E = E - DVE_E
SUMS = ACT_E - 1


def after(engine, semaphore, value):
    if isinstance(value, int) and value <= 0:
        return
    engine.wait_ge(semaphore, value)


def fusion_block(nc, x_t, base, posb, sel, w_patch, w_qkv, w_o, w_g, w_in, w_out, ident_d, bias_l_d, bias_r_d,
                 head_mask_d, iota_d, out):
    ctx = ExitStack()
    with ctx:
        def sb(name, shape, dt=F32):
            return ctx.enter_context(nc.sbuf_tensor(name, shape, dt))

        def sem(name):
            return ctx.enter_context(nc.semaphore(name))

        hid = sb("hid", [P, TILES, D])
        feat = sb("feat", [P, DC, B, S])
        feat_flat = feat[:].rearrange("p c b t -> p c (b t)")
        feat_tb = feat[:].rearrange("p c b t -> p c t b")
        ident = sb("ident", [P, P])
        wqkv_hi, wqkv_lo = sb("wqkv_hi", [P, DC, 3 * D], F32R), sb("wqkv_lo", [P, DC, 3 * D], F32R)
        wo_hi, wo_lo = sb("wo_hi", [P, DC, D], F32R), sb("wo_lo", [P, DC, D], F32R)
        wg = sb("wg", [P, DC, 2 * E], F32R)
        wg_hi, wg_lo = wg[:, :, 0:E], wg[:, :, E:2 * E]
        head_mask = sb("head_mask", [P, HC])
        iota = sb("iota", [P, E])
        bias_l = sb("bias_l", [NBIAS, S], BF16)
        bias_r = sb("bias_r", [NBIAS, H * SP1], BF16)
        win_s = sb("win_s", [P, JC, D])
        wout_s = sb("wout_s", [P, JC, D])
        stats = sb("stats", [P, 4, 6])
        mv = sb("mv", [P, 4, 2])
        rstd = sb("rstd", [P, 4])
        root = sb("root", [P, 3, 4])
        normed = sb("normed", [P, 4, D])
        gtmp = sb("gtmp", [P, 8, E])
        gidx = sb("gidx", [P, E], U32)
        psum = ctx.enter_context(nc.psum_tensor("psum", [P, 8, 512], F32))

        w_in_sem = sem("patch_weights_in")
        c_in = sem("constants_in")
        wq_in = sem("attention_weights_in")
        first_base_in, base_in = sem("first_base_in"), sem("base_in")
        class_ready = sem("class_ready")
        x_in = [sem(f"x_in{n}") for n in range(XSLOT // 2)]
        wp_hi_ready, wp_lo_ready = sem("wp_hi_ready"), sem("wp_lo_ready")
        xh_ready, xl_ready = sem("xh_ready"), sem("xl_ready")
        emb_ready, emb_read = sem("emb_ready"), sem("emb_read")
        dve_chain = sem("dve_chain")
        stats1, stats3, aggr_ready = sem("stats1_ready"), sem("stats3_ready"), sem("aggr_ready")
        var_ready, log_ready, guess_ready = sem("var_ready"), sem("log_ready"), sem("guess_ready")
        normed_ready, normed_used = sem("normed_ready"), sem("normed_used")
        feat_ready = sem("feat_ready")
        w_hi_ready, w_lo_ready = sem("w_hi_ready"), sem("w_lo_ready")
        pads_ready = sem("pads_ready")

        exp_in = sem("expert_in")
        xs_hi, xs_lo = sem("xs_hi"), sem("xs_lo")
        proj_ready = sem("proj_ready")
        proj_hi = sem("proj_hi")
        q_ready, k_ready, vt_ready = sem("q_ready"), sem("k_ready"), sem("vt_ready")
        vraw_ready, v_ready = sem("vraw_ready"), sem("v_ready")
        ot_ready, me_ready, me_hi_done, me_done = sem("ot_ready"), sem("me_ready"), sem("me_hi_done"), sem("me_done")
        ot_done = sem("ot_done")
        kbd_ready = sem("kbd_ready")
        s_ready, max_done, shifted_ready = sem("s_ready"), sem("max_done"), sem("shifted_ready")
        probs_ready, pt_ready, pt_hi_done, pt_lo_done = (sem("probs_ready"), sem("pt_ready"), sem("pt_hi_done"),
                                                         sem("pt_lo_done"))
        pv_ready, otmp_ready, o_read, on_ready = sem("pv_ready"), sem("otmp_ready"), sem("o_read"), sem("on_ready")

        of_hi, of_lo = sem("of_hi"), sem("of_lo")
        wo_ready, mid_ready = sem("wo_ready"), sem("mid_ready")
        n2_ready, x2t_ready, x2_hi, x2_lo = sem("n2_ready"), sem("x2t_ready"), sem("x2_hi_done"), sem("x2_lo_done")
        gt_ready, gt_read = sem("gt_ready"), sem("gt_read")
        g_ready, g_read, gd_ready, ge_ready, gates_ready = (sem("g_ready"), sem("g_read"), sem("gd_ready"),
                                                            sem("ge_ready"), sem("gates_ready"))
        moe_ready, moe_read = sem("moe_ready"), sem("moe_read")
        scaled_ready, part_ready, sum_ready = sem("scaled_ready"), sem("part_ready"), sem("sum_ready")
        out_done = sem("out_done")

        early = ExitStack()
        xs = early.enter_context(nc.sbuf_tensor("xs", [P, XSLOT, KP, P], F32))
        wp = win_s[:, 0:KP]
        xh = early.enter_context(nc.sbuf_tensor("xh", [P, XSLOT, KP, P], F32R))
        xl = early.enter_context(nc.sbuf_tensor("xl", [P, XSLOT, KP, P], F32R))
        wp_hi = early.enter_context(nc.sbuf_tensor("wp_hi", [P, KP, D], F32R))
        wp_lo = early.enter_context(nc.sbuf_tensor("wp_lo", [P, KP, D], F32R))
        posb_s = early.enter_context(nc.sbuf_tensor("posb_s", [3, PATCH_TILES + 1, D], F32))
        sel_s = early.enter_context(nc.sbuf_tensor("sel_s", [3, 2, P], F32))
        raw_qkv = early.enter_context(nc.sbuf_tensor("raw_qkv", [P, DC, 3 * D], F32))
        raw_o = early.enter_context(nc.sbuf_tensor("raw_o", [P, DC, D], F32))
        raw_g = early.enter_context(nc.sbuf_tensor("raw_g", [P, DC, E], F32))
        early.close()
        me_hi, me_lo = sb("me_hi", [P, DC, E, D], F32R), sb("me_lo", [P, DC, E, D], F32R)
        late = ExitStack()

        def lsb(name, shape, dt=F32):
            return late.enter_context(nc.sbuf_tensor(name, shape, dt))

        of_h, of_l = lsb("of_h", [P, 2, DC, P], F32R), lsb("of_l", [P, 2, DC, P], F32R)
        x2_h, x2_l = lsb("x2_h", [P, 2, DC, P], F32R), lsb("x2_l", [P, 2, DC, P], F32R)
        logits = lsb("logits", [2 * E, P])
        scaled = lsb("scaled", [P, ACT_E, D])
        part = lsb("part", [P, 2, D])
        late.close()
        mid = ExitStack()

        def msb(name, shape, dt=F32):
            return mid.enter_context(nc.sbuf_tensor(name, shape, dt))

        xg_hi, xg_lo = msb("xg_hi", [P, DC, GT], F32R), msb("xg_lo", [P, DC, GT], F32R)
        qt_hi, qt_lo = msb("qt_hi", [P, 2, DC, GT], F32R), msb("qt_lo", [P, 2, DC, GT], F32R)
        kt_hi, kt_lo = msb("kt_hi", [P, 2, DC, GS, SP1], F32R), msb("kt_lo", [P, 2, DC, GS, SP1], F32R)
        vt = msb("vt", [P, DC, GT])
        vraw = normed[0:S].rearrange("p (f s) (h d) -> p f s h d", f=2, h=H)
        v2 = msb("v2", [S, 2, GS, H, VW], F32R)
        kbd_hi, kbd_lo = msb("kbd_hi", [P, DC, HC, SP1], F32R), msb("kbd_lo", [P, DC, HC, SP1], F32R)
        rowmax = msb("rowmax", [S, 2, HC])
        probs = msb("probs", [S, 2, HC * SP1])
        pt_hi, pt_lo = msb("pt_hi", [S, 2, HC, SP1], F32R), msb("pt_lo", [S, 2, HC, SP1], F32R)
        otmp = msb("otmp", [S, HC, HD])
        osum = msb("osum", [S, HC, HD])
        rden = msb("rden", [S, 2, HC])
        o_nat = msb("o_nat", [S, D])
        mid.close()

        block = ctx.enter_context(nc.Block())

        PAIRS = TILES // 2
        PATCH_PAIRS = PATCH_TILES // 2
        QUADS = PATCH_PAIRS
        LAST = TILES - 1

        def token_columns(view, pair, j):
            if isinstance(pair, int):
                tile = 2 * pair + j
                if tile == PATCH_TILES:
                    return view[:, :, 0:NPATCH + 2:NPATCH + 1, :]
                if tile == LAST:
                    return view[:, :, S - 1:S, :]
                first = 2 * tile + (1 if tile < PATCH_TILES else 0)
                return view[:, :, first:first + 2, :]
            raise ValueError(pair)

        def looped_columns(view, pair, j, patch):
            return view[:, :, bass.ds(pair * 4 + 2 * j + (1 if patch else 0), 2), :]

        def pairs(engine, step):
            step(0, lambda v, j: token_columns(v, 1, j))
            with engine.Fori(1, PATCH_PAIRS - 1) as n:
                step(n, lambda v, j: looped_columns(v, n + 1, j, True))
            step(PATCH_PAIRS - 1, lambda v, j: token_columns(v, PATCH_PAIRS, j))
            with engine.Fori(PATCH_PAIRS, PAIRS - 1) as n:
                step(n, lambda v, j: looped_columns(v, n + 1, j, False))
            step(PAIRS - 1, lambda v, j: token_columns(v, PAIRS, j))

        E_BANK, T_BANK, CLASS_BANK = 0, 3, 7
        ROUNDS = PATCH_TILES // XSLOT
        PB = XSLOT // 2

        def embed_bank(slot):
            return psum[:, E_BANK + slot, :].rearrange("p (j d) -> p j d", j=2)

        def turned_bank(text):
            return psum[:, T_BANK + text, :].rearrange("p (c j r) -> p c j r", c=DC, j=2)

        PT_BANK, O_BANK, M_BANK = 4, 6, 7
        M = psum[:, M_BANK, :]

        def projection_bank(g, step):
            return psum[:, step, :] if isinstance(g, int) and g == 0 else M

        def last_bank_free(pe, g, kind, step, last_group=False):
            order = []
            for at in range(STEPS):
                if at % 2 and not (isinstance(g, int) and g == 0 and at == 1):
                    order.append(("out", at))
                if at == EXPERT_STEP:
                    order.append(("expert", at))
                if not last_group:
                    order.append(("proj", at))
            at = order.index((kind, step)) if kind else len(order)
            if at:
                kind, step = order[at - 1]
                nxt = g + 1
            else:
                kind, step, nxt = "proj", STEPS - 1, g
            if kind == "out":
                pe.wait_ge(ot_done, g * GS + step // 2)
            elif kind == "expert":
                pe.wait_ge(me_done, g + 1)
            else:
                projected(pe, nxt, step)

        def projected(pe, g, step):
            semaphore = (q_ready, k_ready, vt_ready, vraw_ready)[step // 2]
            pe.wait_ge(semaphore, g * 2 + (step % 2 + 1))

        def group_pairs(engine, group):
            with engine.Fori(0, (GROUPS - 2) // 2) as r:
                group(r * 2 + 1, 1, r)
                group(r * 2 + 2, 0, r + 1)

        def group_columns(g):
            if isinstance(g, int):
                return feat_flat[:, :, g * GT:(g + 1) * GT]
            return feat_flat[:, :, bass.ds(g * GT, GT)]

        def sample_columns(sample):
            if isinstance(sample, int):
                return feat_flat[:, :, sample * S:(sample + 1) * S]
            return feat_flat[:, :, bass.ds(sample * S, S)]

        def me_slice(t, e, half):
            if isinstance(e, int):
                return t[:, half, e, :]
            return t[:, half, bass.ds(e, 1), :].rearrange("p o d -> p (o d)")

        def pt_banks():
            return psum[0:S, PT_BANK:PT_BANK + 2, 0:QUAD * SP1].rearrange("p b (h q) -> p b h q", q=SP1)[:, :, :, 0:S]

        def o_bank():
            return psum[0:S, O_BANK, 0:HC * VW].rearrange("p (h v) -> p h v", v=VW)

        def hid_tile(n, j, rows=P):
            if isinstance(n, int):
                return hid[0:rows, 2 * n + j, :]
            return hid[0:rows, bass.ds(n * 2 + j, 1), :].rearrange("p o d -> p (o d)")

        @block.sync
        def _(sp):
            def load_x(n):
                sp.dma_start(xs[:, 2 * n:2 * n + 2], x_t[2 * n:2 * n + 2].rearrange("i p c t -> p i c t")
                             ).then_inc(x_in[n], 16)

            sp.dma_start(wp, w_patch).then_inc(w_in_sem, 16)
            sp.dma_start(posb_s[:], posb).then_inc(w_in_sem, 16)
            sp.dma_start(sel_s[:], sel).then_inc(w_in_sem, 16)
            load_x(0)
            sp.dma_start(hid[:, PATCH_TILES:PATCH_TILES + 2, :], base[0:2 * P].rearrange("(i p) d -> p i d", p=P)
                         ).then_inc(first_base_in, 16)
            sp.dma_start(ident[:], ident_d).then_inc(c_in, 16)
            sp.dma_start(head_mask[:], head_mask_d).then_inc(c_in, 16)
            sp.dma_start(iota[:], iota_d).then_inc(c_in, 16)
            sp.dma_start(bias_l[:], bias_l_d).then_inc(c_in, 16)
            sp.dma_start(bias_r[:], bias_r_d).then_inc(c_in, 16)
            load_x(1)
            sp.dma_start(raw_qkv[:], w_qkv).then_inc(wq_in, 16)
            sp.dma_start(raw_o[:], w_o).then_inc(wq_in, 16)
            sp.dma_start(raw_g[:], w_g).then_inc(wq_in, 16)
            sp.dma_start(hid[:, PATCH_TILES + 2:LAST, :], base[2 * P:(LAST - PATCH_TILES) * P].rearrange(
                "(i p) d -> p i d", p=P)).then_inc(base_in, 16)
            sp.dma_start(hid[0:B, LAST, :], base[(LAST - PATCH_TILES) * P:]).then_inc(base_in, 16)
            load_x(2)
            sp.wait_ge(wp_lo_ready, 1)
            sp.dma_start(win_s[:], w_in[0]).then_inc(exp_in, 16)
            sp.dma_start(wout_s[:], w_out[0]).then_inc(exp_in, 16)
            with sp.Fori(1, PATCH_TILES // XSLOT) as r:
                for n in range(XSLOT // 2):
                    sp.wait_ge(xl_ready, r * XSLOT + (2 * n + 2 - XSLOT))
                    sp.dma_start(xs[:, 2 * n:2 * n + 2],
                                 x_t[bass.ds(r * XSLOT + 2 * n, 2)].rearrange("i p c t -> p i c t")
                                 ).then_inc(x_in[n], 16)
            with sp.Fori(1, E) as e:
                sp.wait_ge(me_ready, e * 2)
                sp.dma_start(win_s[:], w_in[bass.ds(e, 1)].rearrange("e p j d -> p (e j) d")).then_inc(exp_in, 16)
                sp.dma_start(wout_s[:], w_out[bass.ds(e, 1)].rearrange("e p j d -> p (e j) d")).then_inc(exp_in, 16)

            def store(n, token_of):
                for j in range(2):
                    sp.wait_ge(sum_ready, n * 2 + (j + 1))
                    for u in range(2):
                        src = hid[B * u:B * u + B, bass.ds(n * 2 + j, 1), :].rearrange("b o d -> b (o d)")
                        sp.dma_start(out[:, token_of(j, u), :].rearrange("b o d -> b (o d)"), src
                                     ).then_inc(out_done, 16)

            with sp.Fori(0, PATCH_PAIRS) as n:
                store(n, lambda j, u: bass.ds(n * 4 + (2 * j + u + 1), 1))
            store(PATCH_PAIRS, lambda j, u: [slice(0, 1), slice(NPATCH + 1, NPATCH + 2)][u] if j == 0
                  else slice(2 * PATCH_TILES + 2 + u, 2 * PATCH_TILES + 3 + u))
            with sp.Fori(PATCH_PAIRS + 1, PAIRS) as n:
                store(n, lambda j, u: bass.ds(n * 4 + (2 * j + u), 1))
            sp.wait_ge(sum_ready, TILES)
            sp.dma_start(out[:, S - 1, :], hid[0:B, LAST, :]).then_inc(out_done, 16)
            sp.wait_ge(out_done, 16 * S)

        @block.tensor
        def _(pe):
            mm = nc.tensor.matmul

            def mm3(dst, l_hi, l_lo, r_hi, r_lo, start, stop):
                mm(dst, l_hi, r_hi, start=start, stop=False)
                mm(dst, l_lo, r_hi, start=False, stop=False)
                return mm(dst, l_hi, r_lo, start=False, stop=stop)

            def position(tile):
                if isinstance(tile, int):
                    return posb_s[:, tile, :]
                return posb_s[:, bass.ds(tile, 1), :].rearrange("p o d -> p (o d)")

            def embed(n, slot):
                after(pe, emb_read, n - (PB - 1))
                for j in range(2):
                    dst = embed_bank(slot)[:, j, :]
                    mm(dst, sel_s[:, 0, :], position(n * 2 + j), start=True, stop=False)
                    pe.wait_ge(xl_ready, n * 2 + (j + 1))
                    for c in range(KP):
                        last = mm3(dst, xh[:, 2 * slot + j, c, :], xl[:, 2 * slot + j, c, :],
                                   wp_hi[:, c, :], wp_lo[:, c, :], False, c == KP - 1)
                last.then_inc(emb_ready, 1)

            def turn(n, others=(P, P)):
                pe.wait_ge(normed_ready, n + 1)
                after(pe, feat_ready, n)
                for j, r in enumerate((P, P) + others):
                    for c in range(DC):
                        last = nc.tensor.transpose(turned_bank(j // 2)[:, c, j % 2, 0:r],
                                                   normed[0:r, j, c * P:(c + 1) * P], ident[0:r, 0:r])
                last.then_inc(normed_used, 1)

            pe.wait_ge(w_in_sem, 48)
            mm(psum[:, CLASS_BANK, 0:D], sel_s[:, 1, :], position(PATCH_TILES), start=True, stop=True
               ).then_inc(class_ready, 1)
            pe.wait_ge(wp_lo_ready, 1)
            for n in range(PB):
                embed(n, n)
                if n == 0:
                    pe.wait_ge(c_in, 80)
                else:
                    turn(n - 1)
            with pe.Fori(1, ROUNDS) as r:
                for n in range(PB):
                    embed(r * PB + n, n)
                    turn(r * PB + (n - 1))
            turn(QUADS - 1, (B,))

            def project(g, m):
                if m == 0:
                    pe.wait_ge(xs_lo, g + 1)
                for c in range(DC):
                    w = slice(m * P, (m + 1) * P)
                    last = mm3(projection_bank(g, m)[:, 0:GT], wqkv_hi[:, c, w], wqkv_lo[:, c, w], xg_hi[:, c, :], xg_lo[:, c, :],
                               c == 0, c == DC - 1)
                last.then_inc(proj_ready, 1)

            def turn_v(g, half):
                bank = projection_bank(g, 3 * DC + half)
                pe.wait_ge(vt_ready, g * 2 + 2)
                for s in range(2):
                    for c in range(DC):
                        t0 = (2 * half + s) * S
                        last = nc.tensor.transpose(bank[0:S, s * D + c * P:s * D + (c + 1) * P],
                                                   vt[:, c, t0:t0 + S], ident[:])
                last.then_inc(proj_ready, 1)

            def misc(g, step):
                if step < 3 * DC:
                    project(g, step)
                else:
                    turn_v(g, step - 3 * DC)

            def scores(par, step, s):
                c, sample = step % DC, step // DC
                pe.wait_ge(kbd_ready, s + 1)
                after(pe, probs_ready, s - 1)
                for quad in range(HC // QUAD):
                    dst = psum[0:S, 2 * c + quad, 0:QUAD * SP1]
                    lhs = slice(sample * S, (sample + 1) * S)
                    hs = slice(quad * QUAD, (quad + 1) * QUAD)
                    b0 = (c * HC + quad * QUAD) * SP1
                    mm(dst, bias_l[:], bias_r[:, b0:b0 + QUAD * SP1], start=True, stop=False)
                    last = mm3(dst, qt_hi[:, par, c, lhs], qt_lo[:, par, c, lhs],
                               kbd_hi[:, c, hs, :].rearrange("p h k -> p (h k)"),
                               kbd_lo[:, c, hs, :].rearrange("p h k -> p (h k)"), False, True)
                last.then_inc(s_ready, 1)

            def turn_probs(step, s):
                c = step % DC
                pe.wait_ge(probs_ready, s + 1)
                after(pe, pt_lo_done, s)
                for h in range(HC):
                    q0 = (h % QUAD) * SP1
                    last = nc.tensor.transpose(psum[0:S, PT_BANK + h // QUAD, q0:q0 + S],
                                               probs[:, c, h * SP1:h * SP1 + S], ident[0:S, 0:S])
                last.then_inc(pt_ready, 1)

            def weigh(par, step, s):
                c, sample = step % DC, step // DC
                pe.wait_ge(pt_lo_done, s + 1)
                after(pe, o_read, s)
                for h in range(HC):
                    dst = psum[0:S, O_BANK, h * VW:(h + 1) * VW]
                    rhs = v2[:, par, sample, c * HC + h, :]
                    mm(dst, pt_hi[:, c, h, 0:S], rhs, start=True, stop=False)
                    last = mm(dst, pt_lo[:, c, h, 0:S], rhs, start=False, stop=True)
                last.then_inc(pv_ready, 1)

            def turn_out(sample):
                pe.wait_ge(on_ready, sample * 2 + 2)
                for c in range(DC):
                    last = nc.tensor.transpose(M[:, c * S:(c + 1) * S], o_nat[:, c * P:(c + 1) * P], ident[0:S, 0:S])
                last.then_inc(ot_ready, 1)

            def expert(e, mc):
                pe.wait_ge(exp_in, e * 32 + 32)
                for j in range(JC):
                    last = mm(M[:, 0:D], win_s[:, j, mc * P:(mc + 1) * P], wout_s[:, j, :],
                              start=j == 0, stop=j == JC - 1)
                last.then_inc(me_ready, 1)

            def group(g, par, e, last_group=False):
                for step in range(STEPS):
                    s = g * STEPS + step
                    nxt = (step + 1) % STEPS
                    if not (last_group and step == STEPS - 1):
                        if nxt == 0:
                            pe.wait_ge(q_ready, g * DC + 2 * DC)
                        scores(par if nxt else 1 - par, nxt, s + 1)
                    turn_probs(step, s)
                    if step % 2 and not (isinstance(g, int) and g == 0 and step == 1):
                        last_bank_free(pe, g, "out", step, last_group)
                        turn_out(g * GS + (step // 2 - 1))
                    if step == EXPERT_STEP:
                        last_bank_free(pe, g, "expert", step, last_group)
                        expert(e, par)
                    if not (isinstance(g, int) and g == 0 and step == 0):
                        weigh(par if step else 1 - par, (step - 1) % STEPS, s - 1)
                    if not last_group:
                        last_bank_free(pe, g, "proj", step)
                        misc(g + 1, step)
                    if step == 0:
                        pe.wait_ge(v_ready, g * 2 + 2)

            pe.wait_ge(feat_ready, QUADS)
            pe.wait_ge(w_lo_ready, 3)
            pe.wait_ge(pads_ready, 3)
            for step in range(STEPS):
                misc(0, step)
            pe.wait_ge(q_ready, DC)
            scores(0, 0, 0)
            group(0, 0, 0)
            group_pairs(pe, group)
            group(GROUPS - 1, 1, E - 1, last_group=True)
            weigh(1, STEPS - 1, GROUPS * STEPS - 1)
            last_bank_free(pe, GROUPS - 1, None, None, True)
            turn_out(B - 1)

            pe.wait_ge(ot_done, B)
            pe.wait_ge(me_done, GROUPS)

            def out_projection(i, j, rows=P):
                pe.wait_ge(of_lo, i + 1)
                after(pe, mid_ready, i)
                for c in range(DC):
                    last = mm3(psum[0:rows, 4, 0:D], of_h[:, j, c, 0:rows], of_l[:, j, c, 0:rows],
                               wo_hi[:, c, :], wo_lo[:, c, :], c == 0, c == DC - 1)
                last.then_inc(wo_ready, 1)

            def turn_mid(i, j, rows=P):
                pe.wait_ge(n2_ready, i + 1)
                after(pe, x2_lo, i)
                for c in range(DC):
                    last = nc.tensor.transpose(psum[:, 5, c * P:c * P + rows], normed[0:rows, j, c * P:(c + 1) * P],
                                               ident[0:rows, 0:rows])
                last.then_inc(x2t_ready, 1)

            def gate(i, j, rows=P):
                pe.wait_ge(x2_lo, i + 1)
                after(pe, gt_read, i)
                for c in range(DC):
                    mm(psum[0:2 * E, 6, 0:rows], wg[:, c, :], x2_h[:, j, c, 0:rows], start=c == 0, stop=False)
                for c in range(DC):
                    last = mm(psum[0:E, 6, 0:rows], wg_hi[:, c, :], x2_l[:, j, c, 0:rows], start=False,
                              stop=c == DC - 1)
                last.then_inc(gt_ready, 1)

            def gate_is_out(i):
                pe.wait_ge(gt_read, i + 1)
                after(pe, g_read, i)

            def turn_gate(i, rows=P):
                nc.tensor.transpose(psum[0:rows, 7, 0:2 * E], logits[:, 0:rows], ident[0:2 * E, 0:2 * E]
                                    ).then_inc(g_ready, 1)

            def experts(i, j, e2, rows=P, gate_of=None):
                if 2 * e2 < DVE_E:
                    after(pe, moe_read, i * DVE_E + (2 * e2 + 2 - DVE_E))
                else:
                    after(pe, scaled_ready, i * ACT_E + (2 * e2 + 2 - E))
                for c in range(DC):
                    if c == DC - 1 and gate_of is not None:
                        gate_is_out(gate_of)
                    last = mm3(psum[0:rows, e2, :], x2_h[:, j, c, 0:rows], x2_l[:, j, c, 0:rows],
                               me_hi[:, c, 2 * e2:2 * e2 + 2, :].rearrange("p e d -> p (e d)"),
                               me_lo[:, c, 2 * e2:2 * e2 + 2, :].rearrange("p e d -> p (e d)"),
                               c == 0, c == DC - 1)
                last.then_inc(moe_ready, 1)

            def tile3(i, j, rows=P, rows1=P, rows2=P):
                experts(i, j, 0, rows)
                if rows1:
                    turn_mid(i + 1, 1 - j, rows1)
                experts(i, j, 1, rows)
                if rows2:
                    out_projection(i + 2, j, rows2)
                if rows1:
                    gate(i + 1, 1 - j, rows1)
                experts(i, j, 2, rows, i + 1 if rows1 else None)
                if rows1:
                    turn_gate(i + 1, rows1)
                experts(i, j, 3, rows)

            def pair3(n, columns):
                last_pair = isinstance(n, int) and n == PAIRS - 1
                tile3(n * 2, 0, rows2=B if last_pair else P)
                tile3(n * 2 + 1, 1, rows1=B if last_pair else P, rows2=0 if last_pair else P)

            out_projection(0, 0)
            out_projection(1, 1)
            turn_mid(0, 0)
            gate(0, 0)
            gate_is_out(0)
            turn_gate(0)
            pairs(pe, pair3)
            tile3(LAST, 0, rows=B, rows1=0, rows2=0)

        @block.scalar
        def _(act):
            nc.scalar.preload_act_table_set("natural_log_exp_and_others")

            def copy(dst, src, scale=1.0):
                return nc.scalar.activation(dst, src, ACT.Copy, scale=scale)

            def guess(n, j=0, width=2, rows=P):
                act.wait_ge(var_ready, n + 1)
                v, lg, g = (root[0:rows, k, j:j + width] for k in range(3))
                nc.scalar.activation(lg, v, ACT.Ln).then_inc(log_ready, 1)
                act.wait_ge(log_ready, n + 1)
                nc.scalar.activation(g, lg, ACT.Exp, scale=-0.5).then_inc(guess_ready, 1)

            def embedded(n, slot):
                act.wait_ge(emb_ready, n + 1)
                copy(hid[:, bass.ds(n * 2, 2), :], embed_bank(slot)).then_inc(emb_read, 1)

            def turned(n, patches, others):
                act.wait_ge(normed_used, n + 1)
                copy(patches, turned_bank(0).rearrange("p c j (t b) -> p c (j t) b", b=B))
                for dst, src in others:
                    last = copy(dst, src)
                last.then_inc(feat_ready, 1)

            def turned_whole(n):
                turned(n, feat_tb[:, :, bass.ds(n * 4 + 1, 4), :],
                       [(feat_tb[:, :, bass.ds(n * 4 + 4 * PATCH_PAIRS, 4), :],
                         turned_bank(1).rearrange("p c j (t b) -> p c (j t) b", b=B))])

            def split_x(n, slot, loads):
                act.wait_ge(x_in[slot], loads * 16)
                after(act, emb_ready, n - (PB - 1))
                for j in range(2):
                    copy(xh[:, 2 * slot + j], xs[:, 2 * slot + j]).then_inc(xh_ready, 1)

            act.wait_ge(w_in_sem, 48)
            copy(wp_hi[:], wp).then_inc(wp_hi_ready, 1)
            for n in range(PB):
                split_x(n, n, 1)
                if n:
                    embedded(n - 1, n - 1)
                    guess(n - 1, 0, 4)
            turned(0, feat_tb[:, :, 1:5, :],
                   [(token_columns(feat_tb, PATCH_PAIRS, j),
                     turned_bank(1)[:, :, j, :].rearrange("p c (t b) -> p c t b", b=B)) for j in range(2)])
            act.wait_ge(wq_in, 48)
            for dst, src in ((wqkv_hi[:], raw_qkv), (wo_hi[:], raw_o), (wg_hi, raw_g)):
                copy(dst, src[:]).then_inc(w_hi_ready, 1)
            with act.Fori(1, ROUNDS) as r:
                for n in range(PB):
                    split_x(r * PB + n, n, r + 1)
                    embedded(r * PB + (n - 1), (n - 1) % PB)
                    turned_whole(r * PB + (n - 2))
                    guess(r * PB + (n - 1), 0, 4)
            embedded(QUADS - 1, PB - 1)
            turned_whole(QUADS - 2)
            guess(QUADS - 1, 0, 4)
            turned(QUADS - 1, feat_tb[:, :, 4 * QUADS - 3:4 * QUADS + 1, :],
                   [(feat_tb[:, :, S - 1, :], turned_bank(1)[:, :, 0, 0:B])])

            def misc(g, par, step):
                bank = projection_bank(g, step)
                if step < 2 * DC:
                    act.wait_ge(proj_ready, g * STEPS + (step + 1))
                    if step < DC:
                        copy(qt_hi[:, par, step, :], bank[:, 0:GT], HD ** -0.5).then_inc(proj_hi, 1)
                    else:
                        copy(kt_hi[:, par, step - DC, :, 0:S], bank[:, 0:GT].rearrange("p (s t) -> p s t", s=GS)).then_inc(proj_hi, 1)
                elif step < 3 * DC:
                    act.wait_ge(proj_ready, g * STEPS + (step + 1))
                    copy(vt[:, step - 2 * DC, :], bank[:, 0:GT]).then_inc(vt_ready, 1)
                else:
                    act.wait_ge(proj_ready, g * STEPS + (step + 1))
                    half = step - 3 * DC
                    after(act, v_ready, g * 2 + (half - 1))
                    v = bank[0:S, :].rearrange("p (s h d) -> p s h d", s=2, h=H)
                    copy(v2[:, par, 2 * half:2 * half + 2, :, 0:HD], v)
                    copy(vraw[:, half], v).then_inc(vraw_ready, 1)

            def exponentials(step, s):
                c = step % DC
                act.wait_ge(max_done, s + 1)
                after(act, pt_ready, s - 1)
                for h in range(QUAD):
                    nc.scalar.activation(probs[:, c, (QUAD + h) * SP1:(QUAD + h) * SP1 + S],
                                         psum[0:S, 2 * c + 1, h * SP1:h * SP1 + S], ACT.Exp,
                                         bias=rowmax[:, c, QUAD + h:QUAD + h + 1])
                act.wait_ge(shifted_ready, s + 1)
                quad = probs[:, c, 0:QUAD * SP1]
                nc.scalar.activation(quad, quad, ACT.Exp).then_inc(probs_ready, 1)

            def probs_hi(step, s):
                c = step % DC
                act.wait_ge(pt_ready, s + 1)
                after(act, pv_ready, s - 1)
                copy(pt_hi[:, c, :, 0:S].rearrange("p (b h) q -> p b h q", b=2), pt_banks()).then_inc(pt_hi_done, 1)

            def out_low(s):
                act.wait_ge(pv_ready, s + 1)
                after(act, o_read, s)
                copy(otmp[:], o_bank()[:, :, HD:2 * HD]).then_inc(otmp_ready, 1)

            def out_turned(sample):
                act.wait_ge(ot_ready, sample + 1)
                copy(sample_columns(sample), M[:, 0:DC * S].rearrange("p (c t) -> p c t", c=DC)
                     ).then_inc(ot_done, 1)

            def expert(g, e, par):
                act.wait_ge(me_ready, g + 1)
                copy(me_slice(me_hi, e, par), M[:, 0:D]).then_inc(me_hi_done, 1)

            def group(g, par, e, last_group=False):
                for step in range(STEPS):
                    s = g * STEPS + step
                    probs_hi(step, s)
                    if step % 2 and not (isinstance(g, int) and g == 0 and step == 1):
                        out_turned(g * GS + (step // 2 - 1))
                    if not (last_group and step == STEPS - 1):
                        exponentials((step + 1) % STEPS, s + 1)
                    if step == 0 and not (last_group or isinstance(g, int) and g == 0):
                        after(act, proj_ready, g * STEPS + (3 * DC))
                        copy(xg_hi[:], group_columns(g + 1)).then_inc(xs_hi, 1)
                    if step == EXPERT_STEP:
                        expert(g, e, par)
                    if not (isinstance(g, int) and g == 0 and step == 0):
                        out_low(s - 1)
                    if not last_group:
                        misc(g + 1, 1 - par, step)

            act.wait_ge(feat_ready, QUADS)
            act.wait_ge(w_lo_ready, 3)
            act.wait_ge(pads_ready, 3)
            copy(xg_hi[:], group_columns(0)).then_inc(xs_hi, 1)
            for step in range(STEPS):
                if step == 3 * DC:
                    act.wait_ge(proj_ready, 3 * DC)
                    copy(xg_hi[:], group_columns(1)).then_inc(xs_hi, 1)
                misc(0, 0, step)
            exponentials(0, 0)
            group(0, 0, 0)
            group_pairs(act, group)
            group(GROUPS - 1, 1, E - 1, last_group=True)
            out_low(GROUPS * STEPS - 1)
            out_turned(B - 1)

            def spread(i, j, src):
                after(act, wo_ready, i - 1)
                copy(of_h[:, j].rearrange("p c (t b) -> p c t b", b=B)[:, :, 0:src.shape[2], :], src
                     ).then_inc(of_hi, 1)

            def mid_hi(i, j, rows=P):
                act.wait_ge(x2t_ready, i + 1)
                after(act, moe_ready, i * 4 - 4)
                copy(x2_h[:, j, :, 0:rows], psum[:, 5, 0:D].rearrange("p (c r) -> p c r", c=DC)[:, :, 0:rows]
                     ).then_inc(x2_hi, 1)

            def gate_out(i, rows=P):
                act.wait_ge(gt_ready, i + 1)
                after(act, g_ready, i)
                copy(logits[:, 0:rows], psum[0:2 * E, 6, 0:rows]).then_inc(gt_read, 1)

            def gate_exp(i, rows=P):
                act.wait_ge(gd_ready, i + 1)
                nc.scalar.activation(gtmp[0:rows, 2, 1:2], gtmp[0:rows, 2, 0:1], ACT.Exp).then_inc(ge_ready, 1)

            def scale(i, j, e2, rows=P):
                act.wait_ge(moe_ready, i * 4 + (e2 + 1))
                act.wait_ge(gates_ready, i + 1)
                pair = e2 - DVE_E // 2
                after(act, part_ready, i * SUMS + (max(2 * pair, 1) - SUMS))
                for e in (2 * e2, 2 * e2 + 1):
                    nc.scalar.activation(scaled[0:rows, e - DVE_E, :],
                                         psum[0:rows, e2, (e % 2) * D:(e % 2 + 1) * D], ACT.Copy,
                                         scale=gtmp[0:rows, 6 + j, e:e + 1]).then_inc(scaled_ready, 1)

            def tile3(i, j, rows=P, rows1=P, rows2=P, ahead=None):
                if ahead is not None:
                    spread(i + 2, j, ahead)
                if rows1:
                    mid_hi(i + 1, 1 - j, rows1)
                scale(i, j, 1, rows)
                if rows1:
                    gate_out(i + 1, rows1)
                if rows2:
                    guess(i + (QUADS + 2), j, 1, rows2)
                scale(i, j, 2, rows)
                if rows1:
                    gate_exp(i + 1, rows1)
                scale(i, j, 3, rows)

            def pair3(n, columns):
                last_pair = isinstance(n, int) and n == PAIRS - 1
                tile3(n * 2, 0, rows2=B if last_pair else P, ahead=columns(feat_tb, 0))
                tile3(n * 2 + 1, 1, rows1=B if last_pair else P, rows2=0 if last_pair else P,
                      ahead=None if last_pair else columns(feat_tb, 1))

            act.wait_ge(me_done, GROUPS)
            act.wait_ge(ot_done, B)
            for j in range(2):
                spread(j, j, token_columns(feat_tb, 0, j))
            guess(QUADS, 0, 1)
            mid_hi(0, 0)
            gate_out(0)
            gate_exp(0)
            guess(QUADS + 1, 1, 1)
            pairs(act, pair3)
            tile3(LAST, 0, rows=B, rows1=0, rows2=0)

        @block.gpsimd
        def _(pool):
            def split_x(n, slot):
                for j in range(2):
                    pool.wait_ge(xh_ready, n * 2 + (j + 1))
                    nc.gpsimd.tensor_tensor(out=xl[:, 2 * slot + j], in0=xs[:, 2 * slot + j],
                                            in1=xh[:, 2 * slot + j], op=ALU.subtract).then_inc(xl_ready, 1)

            pool.wait_ge(xl_ready, 2)
            for n in range(1, PB):
                split_x(n, n)
            with pool.Fori(1, ROUNDS) as r:
                for n in range(PB):
                    split_x(r * PB + n, n)
            pool.wait_ge(w_hi_ready, 3)
            for lo, raw, hi in ((wqkv_lo[:], raw_qkv, wqkv_hi[:]), (wo_lo[:], raw_o, wo_hi[:]), (wg_lo, raw_g, wg_hi)):
                nc.gpsimd.tensor_tensor(out=lo, in0=raw[:], in1=hi, op=ALU.subtract).then_inc(w_lo_ready, 1)
            pool.wait_ge(feat_ready, QUADS)
            pool.wait_ge(w_lo_ready, 3)
            nc.gpsimd.memset(kt_hi[:, :, :, :, S:SP1].bitcast(F32), 0.0).then_inc(pads_ready, 1)
            nc.gpsimd.memset(kt_lo[:, :, :, :, S:SP1].bitcast(F32), 0.0).then_inc(pads_ready, 1)
            nc.gpsimd.memset(v2[:, :, :, :, 2 * HD:VW].bitcast(F32), 1.0).then_inc(pads_ready, 1)
            pool.wait_ge(pads_ready, 3)
            pool.wait_ge(c_in, 80)

            def spread_keys(g, par, step, s, v=None):
                c, sample = step % DC, step // DC
                if sample == 0:
                    pool.wait_ge(k_ready, g * DC + DC)
                after(pool, s_ready, s - 1)
                mask = head_mask[:].rearrange("p (h o) -> p h o", o=1).to_broadcast([P, HC, SP1])
                for dst, src in ((kbd_hi, kt_hi), (kbd_lo, kt_lo)):
                    if v and src is kt_lo:
                        pool.wait_ge(vraw_ready, v[0] * 2 + (v[2] + 1))
                    k = src[:, par, c, sample, :].rearrange("p (o k) -> p o k", o=1).to_broadcast([P, HC, SP1])
                    last = nc.gpsimd.tensor_tensor(out=dst[:, c], in0=k, in1=mask, op=ALU.mult)
                last.then_inc(kbd_ready, 1)

            def split_v(g, par, half):
                dst = v2[:, par, 2 * half:2 * half + 2]
                nc.gpsimd.tensor_tensor(out=dst[:, :, :, HD:2 * HD], in0=vraw[:, half], in1=dst[:, :, :, 0:HD],
                                        op=ALU.subtract).then_inc(v_ready, 1)

            def group(g, par, e, last_group=False):
                for step in range(STEPS):
                    later = (step + 2) % STEPS
                    s = g * STEPS + step + 2
                    v = None
                    if step == 0 and not (isinstance(g, int) and g == 0):
                        v = (g, par, 1)
                    if step == STEPS - 1 and not last_group:
                        v = (g + 1, 1 - par, 0)
                    if step + 2 < STEPS:
                        spread_keys(g, par, later, s, v)
                    elif not last_group:
                        spread_keys(g + 1, 1 - par, later, s, v)
                    if v:
                        split_v(*v)

            spread_keys(0, 0, 0, 0)
            spread_keys(0, 0, 1, 1)
            for half in range(2):
                pool.wait_ge(vraw_ready, half + 1)
                split_v(0, 0, half)
            group(0, 0, 0)
            group_pairs(pool, group)
            group(GROUPS - 1, 1, E - 1, last_group=True)

            def spread(i, j, src):
                pool.wait_ge(of_hi, i + 1)
                r = src.shape[2]
                nc.gpsimd.tensor_tensor(out=of_l[:, j].rearrange("p c (t b) -> p c t b", b=B)[:, :, 0:r, :], in0=src,
                                        in1=of_h[:, j].rearrange("p c (t b) -> p c t b", b=B)[:, :, 0:r, :],
                                        op=ALU.subtract).then_inc(of_lo, 1)

            p, q = part[:, 0, :], part[:, 1, :]

            def first_sum(i, rows=P):
                pool.wait_ge(scaled_ready, i * ACT_E + 2)
                after(pool, sum_ready, i)
                nc.gpsimd.tensor_tensor(out=p[0:rows], in0=scaled[0:rows, 0, :], in1=scaled[0:rows, 1, :], op=ALU.add
                                        ).then_inc(part_ready, 1)

            def total(i, tile, rows=P):
                for n in range(1, ACT_E // 2):
                    pool.wait_ge(scaled_ready, i * ACT_E + (2 * n + 2))
                    pool.wait_ge(part_ready, i * SUMS + (2 * n - 1))
                    nc.gpsimd.tensor_tensor(out=q[0:rows], in0=scaled[0:rows, 2 * n, :],
                                            in1=scaled[0:rows, 2 * n + 1, :], op=ALU.add).then_inc(part_ready, 1)
                    pool.wait_ge(part_ready, i * SUMS + 2 * n)
                    nc.gpsimd.tensor_tensor(out=p[0:rows], in0=p[0:rows], in1=q[0:rows], op=ALU.add
                                            ).then_inc(part_ready, 1)
                pool.wait_ge(part_ready, i * SUMS + SUMS)
                pool.wait_ge(moe_read, i * DVE_E + DVE_E)
                nc.gpsimd.tensor_tensor(out=tile, in0=p[0:rows], in1=tile, op=ALU.add).then_inc(sum_ready, 1)

            def pair3(n, columns):
                last_pair = isinstance(n, int) and n == PAIRS - 1
                for j in range(2):
                    if not (last_pair and j):
                        spread(n * 2 + (2 + j), j, columns(feat_tb, j))
                    if j:
                        total(n * 2, hid_tile(n, 0))
                    elif not (isinstance(n, int) and n == 0):
                        total(n * 2 - 1, hid_tile(n - 1, 1))
                    first_sum(n * 2 + j)

            for j in range(2):
                spread(j, j, token_columns(feat_tb, 0, j))
            pairs(pool, pair3)
            total(LAST - 1, hid_tile(PAIRS - 1, 1))
            first_sum(LAST, B)
            total(LAST, hid_tile(PAIRS, 0, B), B)

        @block.vector
        def _(dve):
            tt = nc.vector.tensor_tensor

            def moments(stats_ready, count, total, tiles):
                w = 1 if len(tiles) == 1 else 4
                for j, r, source in tiles:
                    last = nc.vector.bn_stats(stats[0:r, j, :], source)
                last.then_inc(stats_ready, 1)
                dve.wait_ge(c_in, 80)
                dve.wait_ge(stats_ready, count)
                for j, r, source in tiles:
                    last = nc.vector.bn_aggr(mv[0:r, j, :], stats[0:r, j, :])
                last.then_inc(aggr_ready, 1)
                dve.wait_ge(aggr_ready, total + 1)
                j0, r = tiles[0][0], tiles[0][1]
                nc.vector.tensor_scalar_add(root[0:r, 0, j0:j0 + w], mv[0:r, j0:j0 + w, 1], EPS
                                            ).then_inc(var_ready, 1)

            def normalised(chain, count, tiles, used, done):
                j0, r, w = tiles[0][0], tiles[0][1], 1 if len(tiles) == 1 else 4
                v, g = root[0:r, 0, j0:j0 + w], root[0:r, 2, j0:j0 + w]
                rs = rstd[0:r, j0:j0 + w]
                dve.wait_ge(guess_ready, count + 1)
                tt(out=rs, in0=g, in1=g, op=ALU.mult).then_inc(dve_chain, 1)
                dve.wait_ge(dve_chain, chain + 1)
                nc.vector.scalar_tensor_tensor(out=rs, in0=rs, scalar=-0.5, in1=v, op0=ALU.mult, op1=ALU.mult
                                               ).then_inc(dve_chain, 1)
                dve.wait_ge(dve_chain, chain + 2)
                nc.vector.scalar_tensor_tensor(out=rs, in0=rs, scalar=1.5, in1=g, op0=ALU.add, op1=ALU.mult
                                               ).then_inc(dve_chain, 1)
                dve.wait_ge(dve_chain, chain + 3)
                used()
                for j, r, source in tiles:
                    last = nc.vector.tensor_scalar(normed[0:r, j, :], source, mv[0:r, j, 0:1], rstd[0:r, j:j + 1],
                                                   ALU.subtract, ALU.mult)
                last.then_inc(done, 1)

            def norm1(n, others=(P, P)):
                tiles = [(j, P, hid_tile(n, j)) for j in range(2)]
                tiles += [(2 + j, r, hid_tile(n + PATCH_PAIRS, j, r)) for j, r in enumerate(others)]
                dve.wait_ge(emb_read, n + 1)
                moments(stats1, n + 1, n, tiles)
                normalised(n * 3, n, tiles, lambda: after(dve, normed_used, n), normed_ready)

            dve.wait_ge(wp_hi_ready, 1)
            tt(out=wp_lo[:], in0=wp, in1=wp_hi[:], op=ALU.subtract).then_inc(wp_lo_ready, 1)
            for j in range(2):
                dve.wait_ge(xh_ready, j + 1)
                tt(out=xl[:, j], in0=xs[:, j], in1=xh[:, j], op=ALU.subtract).then_inc(xl_ready, 1)
            dve.wait_ge(class_ready, 1)
            dve.wait_ge(first_base_in, 16)
            dve.wait_ge(c_in, 80)
            tt(out=hid_tile(PATCH_PAIRS, 0, B), in0=psum[0:B, CLASS_BANK, 0:D], in1=hid_tile(PATCH_PAIRS, 0, B),
               op=ALU.add).then_inc(class_ready, 1)
            dve.wait_ge(class_ready, 2)
            norm1(0)
            dve.wait_ge(base_in, 32)
            with dve.Fori(1, QUADS - 1) as n:
                norm1(n)
            norm1(QUADS - 1, (B,))

            def misc(g, par, step):
                bank = projection_bank(g, step)
                if step < DC:
                    dve.wait_ge(proj_hi, g * (2 * DC) + (step + 1))
                    nc.vector.scalar_tensor_tensor(out=qt_lo[:, par, step, :], in0=bank[:, 0:GT], scalar=HD ** -0.5,
                                                   in1=qt_hi[:, par, step, :], op0=ALU.mult, op1=ALU.subtract
                                                   ).then_inc(q_ready, 1)
                    return "q"
                if step < 2 * DC:
                    dve.wait_ge(proj_hi, g * (2 * DC) + (step + 1))
                    tt(out=kt_lo[:, par, step - DC, :, 0:S], in0=bank[:, 0:GT].rearrange("p (s t) -> p s t", s=GS),
                       in1=kt_hi[:, par, step - DC, :, 0:S], op=ALU.subtract).then_inc(k_ready, 1)

            def row_maxima(step, s):
                c = step % DC
                dve.wait_ge(s_ready, s + 1)
                sc = psum[0:S, 2 * c:2 * c + 2, 0:QUAD * SP1].rearrange("p b (h k) -> p b h k", k=SP1)
                mx = rowmax[:, c, :].rearrange("p (b h) -> p b h", b=2)
                after(dve, probs_ready, s - 1)
                nc.vector.tensor_reduce(out=mx, in_=sc[:, :, :, 0:S], op=ALU.max, axis=AX_X, negate=True
                                        ).then_inc(max_done, 1)
                dve.wait_ge(max_done, s + 1)
                after(dve, pt_ready, s - 1)
                tt(out=probs[:, c, 0:QUAD * SP1].rearrange("p (h k) -> p h k", k=SP1), in0=sc[:, 0],
                   in1=mx[:, 0].rearrange("p (h o) -> p h o", o=1).to_broadcast([S, QUAD, SP1]), op=ALU.add
                   ).then_inc(shifted_ready, 1)

            def probs_lo(step, s):
                c = step % DC
                dve.wait_ge(pt_hi_done, s + 1)
                tt(out=pt_lo[:, c, :, 0:S].rearrange("p (b h) q -> p b h q", b=2), in0=pt_banks(),
                   in1=pt_hi[:, c, :, 0:S].rearrange("p (b h) q -> p b h q", b=2), op=ALU.subtract
                   ).then_inc(pt_lo_done, 1)

            def normalise(step, s, sample_turned):
                c = step % DC
                dve.wait_ge(otmp_ready, s + 1)
                after(dve, on_ready, s)
                nc.vector.reciprocal(rden[:, c, :], o_bank()[:, :, 2 * HD])
                tt(out=osum[:], in0=o_bank()[:, :, 0:HD], in1=otmp[:], op=ALU.add).then_inc(o_read, 1)
                dve.wait_ge(o_read, s + 1)
                if sample_turned is not None:
                    after(dve, ot_ready, sample_turned)
                tt(out=o_nat[:, c * P:(c + 1) * P].rearrange("p (h d) -> p h d", h=HC), in0=osum[:],
                   in1=rden[:, c, :].rearrange("p (h o) -> p h o", o=1).to_broadcast([S, HC, HD]), op=ALU.mult
                   ).then_inc(on_ready, 1)

            def expert(g, e, par):
                dve.wait_ge(me_hi_done, g + 1)
                tt(out=me_slice(me_lo, e, par), in0=M[:, 0:D], in1=me_slice(me_hi, e, par), op=ALU.subtract
                   ).then_inc(me_done, 1)

            def group(g, par, e, last_group=False):
                for step in range(STEPS):
                    s = g * STEPS + step
                    if not (last_group and step == STEPS - 1):
                        row_maxima((step + 1) % STEPS, s + 1)
                    probs_lo(step, s)
                    if step == 0 and not (last_group or isinstance(g, int) and g == 0):
                        dve.wait_ge(xs_hi, g + 2)
                        tt(out=xg_lo[:], in0=group_columns(g + 1), in1=xg_hi[:], op=ALU.subtract).then_inc(xs_lo, 1)
                    if step == EXPERT_STEP:
                        expert(g, e, par)
                    if not (isinstance(g, int) and g == 0 and step == 0):
                        normalise((step - 1) % STEPS, s - 1, g * GS + (step - 1) // 2)
                    if not last_group:
                        misc(g + 1, 1 - par, step)

            dve.wait_ge(xs_hi, 1)
            tt(out=xg_lo[:], in0=group_columns(0), in1=xg_hi[:], op=ALU.subtract).then_inc(xs_lo, 1)
            for step in range(STEPS):
                misc(0, 0, step)
            dve.wait_ge(xs_hi, 2)
            tt(out=xg_lo[:], in0=group_columns(1), in1=xg_hi[:], op=ALU.subtract).then_inc(xs_lo, 1)
            row_maxima(0, 0)
            group(0, 0, 0)
            group_pairs(dve, group)
            group(GROUPS - 1, 1, E - 1, last_group=True)
            normalise(STEPS - 1, GROUPS * STEPS - 1, B - 1)

            base_chain = 3 * QUADS

            def middle(i, j, tile, rows=P):
                dve.wait_ge(wo_ready, i + 1)
                tt(out=tile, in0=psum[0:rows, 4, 0:D], in1=tile, op=ALU.add).then_inc(mid_ready, 1)
                dve.wait_ge(c_in, 80)
                dve.wait_ge(mid_ready, i + 1)
                moments(stats3, i + 1, i + QUADS, [(j, rows, tile)])

            def norm2(i, j, tile, rows=P):
                chain = base_chain if isinstance(i, int) and i == 0 else i * CH + (base_chain - 4)
                normalised(chain, i + QUADS, [(j, rows, tile)], lambda: None, n2_ready)

            CH = 9

            def mid_lo(i, j, rows=P):
                dve.wait_ge(x2_hi, i + 1)
                view = psum[:, 5, 0:D].rearrange("p (c r) -> p c r", c=DC)[:, :, 0:rows]
                tt(out=x2_l[:, j, :, 0:rows], in0=view, in1=x2_h[:, j, :, 0:rows], op=ALU.subtract
                   ).then_inc(x2_lo, 1)

            def link(ins, value):
                ins.then_inc(dve_chain, 1)
                dve.wait_ge(dve_chain, value)

            def top_two(i, j, rows=P):
                r = slice(0, rows)
                dve.wait_ge(g_ready, i + 1)
                nc.vector.tensor_reduce(out=gtmp[r, 0, :], in_=psum[r, 7, 0:2 * E].rearrange("p (f e) -> p e f", f=2),
                                        op=ALU.add, axis=AX_X).then_inc(g_read, 1)
                dve.wait_ge(c_in, 80)
                dve.wait_ge(g_read, i + 1)
                link(nc.vector.max(gtmp[r, 1, :], gtmp[r, 0, :]), i * CH + (base_chain + 4))
                tt(out=gtmp[r, 2, 0:1], in0=gtmp[r, 1, 1:2], in1=gtmp[r, 1, 0:1], op=ALU.subtract
                   ).then_inc(gd_ready, 1)
                link(nc.vector.max_index(gidx[r, :], gtmp[r, 1, :], gtmp[r, 0, :]), i * CH + (base_chain + 5))
                nc.vector.tensor_copy(gtmp[r, 3, 0:2], gidx[r, 0:2])

            def gates(i, j, rows=P):
                r = slice(0, rows)
                chain = i * CH + (base_chain + (0 if isinstance(i, int) and i == LAST else 3))
                dve.wait_ge(ge_ready, i + 1)
                link(nc.vector.tensor_scalar_add(gtmp[r, 4, 0:1], gtmp[r, 2, 1:2], 1.0), chain + 6)
                link(nc.vector.reciprocal(gtmp[r, 4, 1:2], gtmp[r, 4, 0:1]), chain + 7)
                tt(out=gtmp[r, 4, 2:3], in0=gtmp[r, 2, 1:2], in1=gtmp[r, 4, 1:2], op=ALU.mult)
                link(nc.vector.tensor_scalar(gtmp[r, 5, :], iota[r, :], gtmp[r, 3, 0:1], gtmp[r, 4, 1:2],
                                             ALU.is_equal, ALU.mult), chain + 8)
                link(nc.vector.tensor_scalar(gtmp[r, 0, :], iota[r, :], gtmp[r, 3, 1:2], gtmp[r, 4, 2:3],
                                             ALU.is_equal, ALU.mult), chain + 9)
                after(dve, scaled_ready, (i - 1) * ACT_E)
                tt(out=gtmp[r, 6 + j, :], in0=gtmp[r, 5, :], in1=gtmp[r, 0, :], op=ALU.add).then_inc(gates_ready, 1)

            def combine(i, j, tile, e2, rows=P):
                dve.wait_ge(moe_ready, i * 4 + (e2 + 1))
                dve.wait_ge(gates_ready, i + 1)
                for e in (2 * e2, 2 * e2 + 1):
                    if e:
                        dve.wait_ge(moe_read, i * DVE_E + e)
                    nc.vector.scalar_tensor_tensor(out=tile, in0=psum[0:rows, e2, (e % 2) * D:(e % 2 + 1) * D],
                                                   scalar=gtmp[0:rows, 6 + j, e:e + 1], in1=tile,
                                                   op0=ALU.mult, op1=ALU.add).then_inc(moe_read, 1)

            def tile3(n, j, rows=P, rows1=P, rows2=P):
                i = n * 2 + j
                tile = hid_tile(n, j, rows)
                if rows1:
                    mid_lo(i + 1, 1 - j, rows1)
                combine(i, j, tile, 0, rows)
                if rows2:
                    middle(i + 2, j, hid_tile(n + 1, j, rows2), rows2)
                if rows1:
                    top_two(i + 1, 1 - j, rows1)
                if rows2:
                    norm2(i + 2, j, hid_tile(n + 1, j, rows2), rows2)
                if rows1:
                    gates(i + 1, 1 - j, rows1)

            def pair3(n, columns):
                last_pair = isinstance(n, int) and n == PAIRS - 1
                tile3(n, 0, rows2=B if last_pair else P)
                tile3(n, 1, rows1=B if last_pair else P, rows2=0 if last_pair else P)

            dve.wait_ge(ot_done, B)
            middle(0, 0, hid_tile(0, 0))
            norm2(0, 0, hid_tile(0, 0))
            mid_lo(0, 0)
            top_two(0, 0)
            middle(1, 1, hid_tile(0, 1))
            norm2(1, 1, hid_tile(0, 1))
            gates(0, 0)
            pairs(dve, pair3)
            tile3(PAIRS, 0, rows=B, rows1=0, rows2=0)


def constants():
    import numpy as np
    bf = np.dtype("bfloat16")

    def parts(a):
        hi = a.astype(bf)
        mid = (a - hi.astype(np.float32)).astype(bf)
        lo = (a - hi.astype(np.float32) - mid.astype(np.float32)).astype(bf)
        return hi, mid, lo

    slopes = (np.float32(1.0) / np.power(np.float32(256.0), (np.arange(H, dtype=np.float32) + 1) / np.float32(H))
              ).astype(np.float32)
    left = np.zeros((NBIAS, S), bf)
    right = np.zeros((NBIAS, H, SP1), bf)
    left[:S] = np.eye(S)
    q, k = np.arange(S), np.arange(SP1)
    right[:S] = np.where((k[None, :] > q[:, None]) | (k[None, :] >= S), np.float32(-2.0 ** 100), 0)[:, None, :]
    for n, part in enumerate(parts(slopes)):
        left[S + n] = q
        right[S + n] = -part[:, None]
    for n, part in enumerate(parts(slopes[:, None] * k.astype(np.float32)[None, :])):
        left[S + 3 + n] = 1
        right[S + 3 + n] = part
    sel = np.zeros((3, 2, P), np.float32)
    sel[0, :, :B] = 1
    sel[1, :, B:] = 1
    sel[2, 0, :] = 1
    mask = (np.arange(P)[:, None] // HD == np.arange(HC)[None, :]).astype(np.float32)
    iota = np.broadcast_to(np.arange(E, dtype=np.float32), (P, E)).copy()
    return {"sel": sel, "ident": np.eye(P, dtype=np.float32), "bias_l": left, "bias_r": right.reshape(NBIAS, -1),
            "head_mask": mask, "iota": iota}


def kernel(x, txt, L0_tok_W, L0_tok_b, L0_tok_class_token, L0_tok_pos_emb, L0_attn_W_Q, L0_attn_W_K, L0_attn_W_V,
           L0_attn_W_O, L0_ffn_w_gate, L0_ffn_w_in, L0_ffn_w_out):
    import numpy as np
    import concourse.bacc as bacc
    from concourse import mybir as mb
    from concourse.bass_utils import run_bass_kernel_spmd

    x, txt = np.asarray(x), np.asarray(txt)
    n = IMG // PATCH
    pat = x.reshape(B, CIN, n, PATCH, n, PATCH).transpose(1, 3, 5, 2, 4, 0).reshape(KP, P, PATCH_TILES, 2 * B)
    pat = np.ascontiguousarray(pat.transpose(2, 1, 0, 3))
    cls = np.broadcast_to(np.asarray(L0_tok_class_token).reshape(1, 1, D), (1, B, D))
    base = np.concatenate([cls, txt.transpose(1, 0, 2)], axis=0).reshape(-1, D)
    pos = np.asarray(L0_tok_pos_emb).reshape(NPATCH + 1, D)
    rows = np.zeros((2 * PATCH_TILES + 2, D), pos.dtype)
    rows[:NPATCH], rows[NPATCH] = pos[1:], pos[0]
    bias = np.broadcast_to(np.asarray(L0_tok_b).reshape(1, 1, D), (1, PATCH_TILES + 1, D))
    posb = np.concatenate([rows.reshape(PATCH_TILES + 1, 2, D).transpose(1, 0, 2), bias], axis=0)

    def by_row(w):
        return np.ascontiguousarray(w.reshape(-1, P, w.shape[1]).transpose(1, 0, 2))

    wq, wk, wv = (np.asarray(w) for w in (L0_attn_W_Q, L0_attn_W_K, L0_attn_W_V))
    inputs = {
        "x_t": pat, "base": base, "posb": posb,
        "w_patch": by_row(np.asarray(L0_tok_W)),
        "w_qkv": by_row(np.concatenate([wq.T, wk.T, wv.T], axis=1)),
        "w_o": by_row(np.asarray(L0_attn_W_O).T),
        "w_g": by_row(np.asarray(L0_ffn_w_gate).T),
        "w_in": np.asarray(L0_ffn_w_in).reshape(E, P, JC, D),
        "w_out": np.ascontiguousarray(np.asarray(L0_ffn_w_out).transpose(0, 2, 1)).reshape(E, P, JC, D),
    }
    inputs.update(constants())
    order = ["x_t", "base", "posb", "sel", "w_patch", "w_qkv", "w_o", "w_g", "w_in", "w_out", "ident", "bias_l",
             "bias_r", "head_mask", "iota"]
    nc = bacc.Bacc("TRN2", target_bir_lowering=False, num_devices=1)
    arrays, aps = {}, []
    for name in order:
        a = np.ascontiguousarray(inputs[name])
        arrays[f"in_{name}"] = a
        aps.append(nc.dram_tensor(f"in_{name}", a.shape, mb.dt.from_np(a.dtype), kind="ExternalInput").ap())
    out = nc.dram_tensor("out", (B, S, D), F32, kind="ExternalOutput").ap()
    fusion_block(nc, *aps, out)
    r = run_bass_kernel_spmd(nc, [arrays], core_ids=[0])
    return r.results[0]["out"]
```
